# Optimizing a Trainium2 kernel written in Bass

```python
import numpy as np
import jax
import jax.numpy as jnp

def _softmax(x, axis=-1):
    return jax.nn.softmax(x, axis=axis)

def _gelu(x):
    return jax.nn.gelu(x, approximate=True)

def _silu(x):
    return jax.nn.silu(x)

def _sigmoid(x):
    return jax.nn.sigmoid(x)

def _layernorm(x, axis=-1, eps=1e-05):
    m = jnp.mean(x, axis=axis, keepdims=True)
    v = jnp.var(x, axis=axis, keepdims=True)
    return (x - m) / jnp.sqrt(v + eps)

def _scatter_add(tgt, idx, src, axis=0):
    return tgt.at[idx].add(src)

def _segment_sum(src, seg, n):
    return jax.ops.segment_sum(src, seg, n)
kernel_name = 'mk_seq_preln_d1_jaxref_r8_f4f777'

def setup_inputs(seed: int=0):
    np.random.seed(seed)
    _w = jnp.asarray

    def _L0_attn_setup():
        import jax, jax.numpy as jnp
        import numpy as np
        import math
        D = 128
        H = 16
        HEAD_D = D // H
        T = 256
        B = 4
        key = jax.random.key(seed)
        k1, k2, k3 = jax.random.split(key, 3)
        x = jax.random.normal(k1, (B, T, D), dtype=jnp.float32)
        w_attn = jax.random.normal(k2, (D, D + 2 * HEAD_D), dtype=jnp.float32) * (1.0 / math.sqrt(D))
        w_proj = jax.random.normal(k3, (D, D), dtype=jnp.float32) * (1.0 / math.sqrt(D))
        return {'x': x, 'w_attn': w_attn, 'w_proj': w_proj}
    _L0_attn_in = _L0_attn_setup()

    def _L0_ffn_setup():
        import jax, jax.numpy as jnp
        import numpy as np
        DIM = 128
        HEADS = 8
        NUM_EXPERTS = 8192
        NUM_KEYS = 32
        DIM_KEY = 64
        TOPK = 16

        def _rmsnorm(v, g):
            scale = jnp.sqrt(jnp.asarray(v.shape[-1], v.dtype))
            n = jnp.maximum(jnp.linalg.norm(v, axis=-1, keepdims=True), 1e-12)
            return v / n * g * scale
        key = jax.random.key(seed)
        ks = jax.random.split(key, 6)
        B, N = (2, 64)
        x = jax.random.normal(ks[0], (B, N, DIM), dtype=jnp.float32)
        gamma = jnp.ones((DIM,), dtype=jnp.float32)
        wq = jax.random.normal(ks[1], (2 * HEADS * DIM_KEY, DIM), dtype=jnp.float32) * 0.02
        keys = jax.random.normal(ks[2], (HEADS, NUM_KEYS, 2, DIM_KEY), dtype=jnp.float32) * 0.02
        table_down = jax.random.normal(ks[3], (NUM_EXPERTS, DIM), dtype=jnp.float32) * 0.02
        table_up = jax.random.normal(ks[4], (NUM_EXPERTS, DIM), dtype=jnp.float32) * 0.02
        return {'x': x, 'gamma': gamma, 'wq': wq, 'keys': keys, 'table_down': table_down, 'table_up': table_up}
    _L0_ffn_in = _L0_ffn_setup()
    _d = {'L0_attn_x': _L0_attn_in['x'], 'L0_attn_w_attn': _L0_attn_in['w_attn'], 'L0_attn_w_proj': _L0_attn_in['w_proj'], 'L0_ffn_gamma': _L0_ffn_in['gamma'], 'L0_ffn_wq': _L0_ffn_in['wq'], 'L0_ffn_keys': _L0_ffn_in['keys'], 'L0_ffn_table_down': _L0_ffn_in['table_down'], 'L0_ffn_table_up': _L0_ffn_in['table_up']}
    _x0 = _d['L0_attn_x']
    _d['L0_attn_x'] = jax.random.normal(jax.random.fold_in(jax.random.key(seed), 1), (16, 256, 128), dtype=_x0.dtype)
    del _x0
    return _d

def reference(L0_attn_x, L0_attn_w_attn, L0_attn_w_proj, L0_ffn_gamma, L0_ffn_wq, L0_ffn_keys, L0_ffn_table_down, L0_ffn_table_up):

    def _L0_attn_ref(x, w_attn, w_proj):
        import jax, jax.numpy as jnp
        import numpy as np
        import math
        D = 128
        H = 16
        HEAD_D = D // H
        T = 256
        B = 4
        Bv, Tv, _ = x.shape
        qkv = x @ w_attn
        q = qkv[..., :D].reshape(Bv, Tv, H, HEAD_D).transpose(0, 2, 1, 3)
        k = qkv[..., D:D + HEAD_D]
        v = qkv[..., D + HEAD_D:]
        scale = 1.0 / math.sqrt(HEAD_D)
        att = jnp.einsum('bhqd,bkd->bhqk', q, k) * scale
        causal = jnp.tril(jnp.ones((Tv, Tv), dtype=bool))
        att = jnp.where(causal[None, None, :, :], att, -jnp.inf)
        att = jax.nn.softmax(att, axis=-1)
        y = jnp.einsum('bhqk,bkd->bhqd', att, v)
        y = y.transpose(0, 2, 1, 3).reshape(Bv, Tv, D)
        return y @ w_proj

    def _L0_ffn_ref(x, gamma, wq, keys, table_down, table_up):
        import jax, jax.numpy as jnp
        import numpy as np
        DIM = 128
        HEADS = 8
        NUM_EXPERTS = 8192
        NUM_KEYS = 32
        DIM_KEY = 64
        TOPK = 16

        def _rmsnorm(v, g):
            scale = jnp.sqrt(jnp.asarray(v.shape[-1], v.dtype))
            n = jnp.maximum(jnp.linalg.norm(v, axis=-1, keepdims=True), 1e-12)
            return v / n * g * scale
        B, N, D = x.shape
        xn = _rmsnorm(x, gamma)
        gate = xn
        q = gate @ wq.T
        q = q.reshape(B, N, 2, HEADS, DIM_KEY).transpose(2, 0, 1, 3, 4)
        sim = jnp.einsum('pbnhd,hkpd->pbnhk', q, keys)
        sx, ix = jax.lax.top_k(sim[0], TOPK)
        sy, iy = jax.lax.top_k(sim[1], TOPK)
        all_scores = (sx[..., :, None] + sy[..., None, :]).reshape(B, N, HEADS, TOPK * TOPK)
        all_indices = (ix[..., :, None] * NUM_KEYS + iy[..., None, :]).reshape(B, N, HEADS, TOPK * TOPK)
        scores, pk = jax.lax.top_k(all_scores, TOPK)
        indices = jnp.take_along_axis(all_indices, pk, axis=-1)
        wd = table_down[indices]
        wu = table_up[indices]
        h = jnp.einsum('bnd,bnhkd->bnhk', xn, wd)
        h = jax.nn.gelu(h, approximate=False) * jax.nn.softmax(scores, axis=-1)
        out = jnp.einsum('bnhk,bnhkd->bnd', h, wu)
        return out
    x = L0_attn_x
    x = x + _L0_attn_ref(_layernorm(x, axis=-1), L0_attn_w_attn, L0_attn_w_proj)
    x = x + _L0_ffn_ref(_layernorm(x, axis=-1), L0_ffn_gamma, L0_ffn_wq, L0_ffn_keys, L0_ffn_table_down, L0_ffn_table_up)
    return x

_drawn_inputs = setup_inputs


def setup_inputs(seed=0):
    import zlib

    import numpy as np

    out = dict(_drawn_inputs(seed))
    spreads = {'L0_ffn_gamma': (1.0, 0.6)}
    factors = {'L0_ffn_wq': 8.0, 'L0_ffn_keys': 8.0, 'L0_ffn_table_down': 8.0, 'L0_ffn_table_up': 8.0}
    for name, (base, spread) in spreads.items():
        noise = np.random.default_rng([zlib.crc32(name.encode()), seed]).standard_normal(out[name].shape)
        drawn = base * np.exp(spread * noise) if base else spread * noise
        out[name] = jnp.asarray(drawn.astype(out[name].dtype))
    for name, factor in factors.items():
        out[name] = (out[name] * factor).astype(out[name].dtype)
    return out
```

```python
import concourse.bass as bass
from concourse import mybir
from contextlib import ExitStack

FP32 = mybir.dt.float32
BF16 = mybir.dt.bfloat16
ALU = mybir.AluOpType
ACT = mybir.ActivationFunctionType
AX = mybir.AxisListType

P = 128
BATCHES, T, D = 16, 256, 128
TILES = T // P
H, HD = 16, 8
FH, KEYS, DK = 8, 32, 64
EXPERTS = KEYS * KEYS
CH = EXPERTS // P
TOPK = 16
LISTS = 2 * FH
LN_EPS = 1e-5
MASKED = -float(2 ** 100)
LOWEST = -3.0e38
Q_PIECE = (0, 0, 0, 1, 1, 2)
K_PIECE = (0, 1, 2, 0, 1, 0)
STACK = len(Q_PIECE) * HD
PAIR_BLOCKS = ((0, 1, 16), (1, 1, 8), (2, 2, 5), (4, 4, 3), (8, 8, 1))
PAIRS = sum(na * nb for _, na, nb in PAIR_BLOCKS)
BANK = 512
MAX_STEPS = 12


def later(batch):
    return not isinstance(batch, int) or batch > 0


def held(eng, value):
    return value if isinstance(value, int) else eng.to_reg(value)


def build(nc, x, w_attn, w_proj, gamma, wq, keys, down, up, consts, out):
    ctx = ExitStack()
    with ctx:
        def sb(name, shape, dt=FP32):
            return ctx.enter_context(nc.sbuf_tensor(name, shape, dt))

        raised = {}

        def signal(name, per_batch=1):
            sem = ctx.enter_context(nc.semaphore(name))
            raised[sem] = per_batch
            return sem

        def at(sem, batch, n):
            return batch * raised[sem] + n

        def every(sem, batch):
            return at(sem, batch, raised[sem])

        q_scratch = nc.dram_tensor("q_scratch", (P, 3, T), BF16, kind="Internal").ap()

        NC = consts.shape[1]
        ident = sb("ident", [P, P])
        cb = sb("cb", [P, NC], BF16)
        ident_bf = cb[:, 0:P]
        mask_q0 = cb[:, P:P + BANK]
        mask_q1 = cb[:, P + BANK:P + 2 * BANK]
        mask_t0 = cb[:, P + 2 * BANK:P + 3 * BANK]
        mask_t1 = cb[:, P + 3 * BANK:P + 4 * BANK]
        SEL = P + 4 * BANK
        sel_high = cb[:, SEL:SEL + EXPERTS]
        sel_low = [cb[:, SEL + (1 + n) * EXPERTS:SEL + (2 + n) * EXPERTS] for n in range(2)]
        wa = sb("wa", [P, D + 2 * HD])
        wp = sb("wp", [P, D])
        gam = sb("gam", [P, 1])
        wqs = sb("wqs", [DK, LISTS, D])
        keyt = sb("keyt", [DK, LISTS * KEYS])
        wkey = sb("wkey", [P, LISTS * KEYS])
        wdt = sb("wdt", [P, EXPERTS])
        wu = sb("wu", [P, CH, D])

        xin = sb("xin", [P, TILES, D])
        stat1 = sb("stat1", [P, TILES, 6])
        mv1 = sb("mv1", [P, TILES, 2])
        rstd1 = sb("rstd1", [P, TILES])
        half_neg = sb("half_neg", [P, TILES])
        ln_tmp = sb("ln_tmp", [P, TILES])
        xhat = sb("xhat", [P, TILES, D])
        xhat_t = sb("xhat_t", [P, T])
        qk_piece = sb("qk_piece", [P, 3, 2 * T], BF16)
        qk_rest = sb("qk_rest", [P, 2 * T])
        v_next = sb("v_next", [P, TILES, HD])
        q_stack = sb("q_stack", [STACK + 1, H, T], BF16)
        k_stack = sb("k_stack", [STACK + 1, T], BF16)
        v_ones = sb("v_ones", [P, TILES, HD + 1])
        neg_max = sb("neg_max", [P, H, TILES])
        max_t = sb("max_t", [H * TILES, P], BF16)
        probs0 = sb("probs0", [P, H, T])
        probs1 = sb("probs1", [P, H, P])
        recip = sb("recip", [P, TILES, H])
        y = sb("y", [P, TILES, D])
        y_t = sb("y_t", [P, T])
        xres = sb("xres", [P, TILES, D])
        x2 = sb("x2", [P, TILES, D])
        x2_kept = sb("x2_kept", [P, TILES, D])
        stat2 = sb("stat2", [P, TILES, 6])
        mv2 = sb("mv2", [P, TILES, 2])
        bounded = sb("bounded", [P, TILES])
        scale2 = sb("scale2", [P, TILES])
        xn = sb("xn", [P, TILES, D])
        xn_t = sb("xn_t", [P, T])
        sim = sb("sim", [P, TILES, LISTS * KEYS])
        sim_hm = sb("sim_hm", [P, TILES, FH, 2, 2 * KEYS], BF16)
        sim_lo = sb("sim_lo", [P, TILES, LISTS * KEYS], BF16)
        sim_rest = sb("sim_rest", [P, LISTS * KEYS])
        hm_t = sb("hm_t", [P, TILES, FH, P], BF16)
        lo_t = sb("lo_t", [P, TILES, FH // 2, P], BF16)
        top = sb("top", [P, LISTS, TOPK])
        left = sb("left", [P, LISTS, KEYS])
        cand = sb("cand", [P, FH, PAIRS])
        cand_left = sb("cand_left", [P, FH, PAIRS])
        best = sb("best", [P, TILES, FH, TOPK])
        size = sb("size", [P, TILES, FH])
        cut = sb("cut", [P, TILES, FH])
        shifted = sb("shifted", [P, TILES, FH, TOPK])
        exps = sb("exps", [P, TILES, FH, TOPK])
        total = sb("total", [P, TILES, FH])
        log_total = sb("log_total", [P, TILES, FH])
        neg_lse = sb("neg_lse", [P, TILES, FH])
        cut_arg = sb("cut_arg", [P, TILES, FH])
        cut_prob = sb("cut_prob", [P, TILES, FH])
        prob = sb("prob", [P, TILES * FH, EXPERTS])
        acc = sb("acc", [P, TILES, EXPERTS])
        act_t = sb("act_t", [P, CH, T])
        gated_t = sb("gated_t", [P, CH, T])
        fin = sb("fin", [P, TILES, D])
        consts_f = prob[:, :, :].rearrange("p a b -> p (a b)")[:, 0:NC]

        score = [ctx.enter_context(nc.psum_tensor(f"score{n}", [P, EXPERTS], FP32)) for n in range(2)]
        att = [ctx.enter_context(nc.psum_tensor(f"att{n}", [P, BANK], FP32)) for n in range(2)]
        misc = [ctx.enter_context(nc.psum_tensor(f"misc{n}", [P, BANK], FP32)) for n in range(2)]
        av = att[0][:, 0:TILES * H * (HD + 1)].rearrange("p (t h e) -> p t h e", t=TILES, e=HD + 1)

        weights_in = signal("weights_in")
        consts_in = signal("consts_in")
        ones_in = signal("ones_in")
        setup_pool = signal("setup_pool")
        setup_dve = signal("setup_dve")
        wkey_made = signal("wkey_made")
        setup_done = signal("setup_done", 2)
        x_in = signal("x_in", 16)
        ln1_step = signal("ln1_step", 5)
        rstd1_made = signal("rstd1_made")
        xhat_made = signal("xhat_made", 2)
        xhat_tp = signal("xhat_tp")
        xhat_t_made = signal("xhat_t_made")
        qk_made = signal("qk_made")
        v_made = signal("v_made")
        qk_high = signal("qk_high")
        qk_rest_made = signal("qk_rest_made")
        qk_low = signal("qk_low", 2)
        v_next_made = signal("v_next_made")
        scratch_in = signal("scratch_in", 16)
        stack_in = signal("stack_in", 16 * 2 * len(Q_PIECE))
        max_scores = signal("max_scores", MAX_STEPS)
        max_taken = signal("max_taken", MAX_STEPS)
        max_tp = signal("max_tp")
        max_t_made = signal("max_t_made")
        max_row_in = signal("max_row_in", 16)
        att_scores = signal("att_scores", MAX_STEPS)
        att_probs = signal("att_probs", MAX_STEPS)
        v_copied = signal("v_copied")
        av_made = signal("av_made")
        recip_made = signal("recip_made")
        y_made = signal("y_made")
        y_tp = signal("y_tp")
        y_t_made = signal("y_t_made")
        proj_made = signal("proj_made")
        xres_in = signal("xres_in", 16)
        x2_made = signal("x2_made")
        ln2_step = signal("ln2_step", 6)
        scale2_made = signal("scale2_made")
        xn_made = signal("xn_made", 2)
        xn_tp = signal("xn_tp")
        xn_t_made = signal("xn_t_made")
        sim_made = signal("sim_made", 2)
        sim_kept = signal("sim_kept", 2)
        sim_high = signal("sim_high", 2)
        sim_low = signal("sim_low", 6)
        piece_tp = signal("piece_tp", 4)
        piece_t_made = signal("piece_t_made", 4)
        hidden = signal("hidden", 4)
        act_made = signal("act_made", 4)
        SELECT = 3 * LISTS + len(PAIR_BLOCKS) + 1 + 3 * FH + 1
        select_step = signal("select_step", TILES * SELECT)
        shifted_made = signal("shifted_made", 2)
        exps_made = signal("exps_made", 2)
        total_made = signal("total_made", 2)
        log_made = signal("log_made", 2)
        lse_step = signal("lse_step", 2)
        cut_arg_made = signal("cut_arg_made", 2)
        cut_prob_made = signal("cut_prob_made", 2)
        scores_made = signal("scores_made", TILES * FH)
        prob_made = signal("prob_made", TILES * FH)
        prob_masked = signal("prob_masked", TILES * FH)
        acc_added = signal("acc_added", TILES * (FH - 1))
        x2_copied = signal("x2_copied")
        acc_tp = signal("acc_tp", 4)
        gated = signal("gated", 4)
        down_made = signal("down_made")
        fin_made = signal("fin_made")
        out_stored = signal("out_stored", 16)

        block = ctx.enter_context(nc.Block())

        def schedule(eng, prologue, iteration):
            prologue()
            iteration(0, d=False, f=True, a=True, p=True)
            with eng.Fori(1, BATCHES - 2) as i:
                iteration(i, d=True, f=True, a=True, p=True)
            iteration(BATCHES - 2, d=True, f=True, a=True, p=False)
            iteration(BATCHES - 1, d=True, f=True, a=False, p=False)
            iteration(BATCHES, d=True, f=False, a=False, p=False)

        @block.sync
        def _(eng):
            x_v = x.rearrange("b (j p) d -> b p j d", p=P)
            out_v = out.rearrange("b (j p) d -> b p j d", p=P)

            def load_x(b):
                if later(b):
                    value = held(eng, at(xhat_made, b, 0))
                    eng.wait_ge(setup_dve, 1)
                    eng.wait_ge(xhat_made, value)
                eng.dma_start(xin[:, :, :], x_v[b]).then_inc(x_in, 16)

            def load_residual(b):
                if later(b):
                    value = held(eng, at(x2_made, b, 0))
                    eng.wait_ge(setup_dve, 1)
                    eng.wait_ge(x2_made, value)
                eng.dma_start(xres[:, :, :], x_v[b]).then_inc(xres_in, 16)

            def stack_pieces(b):
                value = held(eng, every(qk_low, b))
                eng.wait_ge(setup_dve, 1)
                eng.wait_ge(qk_low, value)
                value = held(eng, every(qk_high, b))
                eng.wait_ge(setup_dve, 1)
                eng.wait_ge(qk_high, value)
                eng.dma_start(q_scratch, qk_piece[:, :, 0:T]).then_inc(scratch_in, 16)
                value = held(eng, every(scratch_in, b))
                eng.wait_ge(setup_dve, 1)
                eng.wait_ge(scratch_in, value)
                if later(b):
                    value = held(eng, at(att_scores, b, 0))
                    eng.wait_ge(setup_dve, 1)
                    eng.wait_ge(att_scores, value)
                view = q_scratch.rearrange("(h d) s t -> s d h t", d=HD)
                for c in range(len(Q_PIECE)):
                    rows = slice(c * HD, (c + 1) * HD)
                    eng.dma_start(q_stack[rows, :, :], view[Q_PIECE[c]]).then_inc(stack_in, 16)
                    eng.dma_start(k_stack[rows, :],
                                  qk_piece[D - 2 * HD:D - HD, K_PIECE[c], T:2 * T]).then_inc(stack_in, 16)
                value = held(eng, every(stack_in, b))
                eng.wait_ge(setup_dve, 1)
                eng.wait_ge(stack_in, value)

            def place_max_row(b):
                value = held(eng, every(max_t_made, b))
                eng.wait_ge(setup_dve, 1)
                eng.wait_ge(max_t_made, value)
                if later(b):
                    value = held(eng, at(att_scores, b, 0))
                    eng.wait_ge(setup_dve, 1)
                    eng.wait_ge(att_scores, value)
                row = q_stack[STACK:STACK + 1, :, :].rearrange("o h (j t) -> o (h j) t", t=P)
                eng.dma_start(row, max_t[:, :]).then_inc(max_row_in, 16)

            def store(b):
                value = held(eng, every(fin_made, b))
                eng.wait_ge(setup_dve, 1)
                eng.wait_ge(fin_made, value)
                eng.dma_start(out_v[b], fin[:, :, :]).then_inc(out_stored, 16)

            def prologue():
                load_x(0)
                eng.dma_start(consts_f, consts).then_inc(consts_in, 16)
                eng.dma_start(ident[:, :], consts[:, 0:P]).then_inc(consts_in, 16)
                for dst, src in ((wa[:, :], w_attn), (wp[:, :], w_proj), (gam[:, :], gamma),
                                 (wqs[:, :, :], wq), (keyt[:, :], keys), (wdt[:, :], down),
                                 (wu[:, :, :], up.rearrange("(c p) d -> p c d", p=P))):
                    eng.dma_start(dst, src).then_inc(weights_in, 16)
                eng.wait_ge(setup_dve, 1)
                eng.dma_start(k_stack[STACK:STACK + 1, :], sel_ones).then_inc(ones_in, 16)
                stack_pieces(0)
                load_x(1)
                load_residual(0)
                place_max_row(0)
                stack_pieces(1)

            sel_ones = cb[0:1, NC - T:NC]

            def iteration(i, d, f, a, p):
                if p:
                    load_x(i + 2)
                if a:
                    load_residual(i + 1)
                    place_max_row(i + 1)
                if d:
                    store(i - 1)
                if p:
                    stack_pieces(i + 2)

            schedule(eng, prologue, iteration)
            value = held(eng, every(out_stored, BATCHES - 1))
            eng.wait_ge(setup_dve, 1)
            eng.wait_ge(out_stored, value)

        @block.gpsimd
        def _(eng):

            def rstd(b):
                eng.wait_ge(ln1_step, every(ln1_step, b))
                if later(b):
                    eng.wait_ge(xhat_made, at(xhat_made, b, 0))
                eng.tensor_tensor(rstd1[:, :], ln_tmp[:, :], half_neg[:, :], ALU.pow).then_inc(rstd1_made, 1)

            def qk_pieces(b):
                value = held(eng, every(qk_rest_made, b))
                eng.wait_ge(setup_pool, 1)
                eng.wait_ge(qk_rest_made, value)
                if later(b):
                    value = held(eng, at(stack_in, b, 0))
                    eng.wait_ge(setup_pool, 1)
                    eng.wait_ge(stack_in, value)
                eng.tensor_copy(qk_piece[:, 1, :], qk_rest[:, :]).then_inc(qk_low, 1)
                value = held(eng, at(qk_low, b, 1))
                eng.wait_ge(setup_pool, 1)
                eng.wait_ge(qk_low, value)
                eng.tensor_tensor(qk_piece[:, 2, :], qk_rest[:, :], qk_piece[:, 1, :],
                                  ALU.subtract).then_inc(qk_low, 1)

            def copy_v(b):
                value = held(eng, every(v_next_made, b))
                eng.wait_ge(setup_pool, 1)
                eng.wait_ge(v_next_made, value)
                if later(b):
                    value = held(eng, at(av_made, b, 0))
                    eng.wait_ge(setup_pool, 1)
                    eng.wait_ge(av_made, value)
                eng.tensor_copy(v_ones[:, :, 0:HD], v_next[:, :, :]).then_inc(v_copied, 1)

            def scale(b):
                eng.wait_ge(ln2_step, every(ln2_step, b))
                if later(b):
                    eng.wait_ge(xn_made, at(xn_made, b, 0))
                eng.tensor_tensor(scale2[:, :], bounded[:, :], half_neg[:, :], ALU.pow).then_inc(scale2_made, 1)

            def copy_x2(b):
                value = held(eng, every(x2_made, b))
                eng.wait_ge(setup_pool, 1)
                eng.wait_ge(x2_made, value)
                if later(b):
                    value = held(eng, at(fin_made, b, 0))
                    eng.wait_ge(setup_pool, 1)
                    eng.wait_ge(fin_made, value)
                eng.tensor_copy(x2_kept[:, :, :], x2[:, :, :]).then_inc(x2_copied, 1)

            def sim_pieces(b, j):
                value = held(eng, at(sim_high, b, j + 1))
                eng.wait_ge(setup_pool, 1)
                eng.wait_ge(sim_high, value)
                value = held(eng, at(sim_kept, b, j + 1))
                eng.wait_ge(setup_pool, 1)
                eng.wait_ge(sim_kept, value)
                if later(b):
                    value = held(eng, at(piece_tp, b, 0))
                    eng.wait_ge(setup_pool, 1)
                    eng.wait_ge(piece_tp, value)
                if j:
                    value = held(eng, at(sim_low, b, 3 * j))
                    eng.wait_ge(setup_pool, 1)
                    eng.wait_ge(sim_low, value)
                v = sim[:, j, :].rearrange("p (h k) -> p h k", h=FH)
                rest = sim_rest[:, :].rearrange("p (h k) -> p h k", h=FH)
                low = sim_lo[:, j, :].rearrange("p (h k) -> p h k", h=FH)
                eng.tensor_tensor(rest, v, sim_hm[:, j, :, 0, :], ALU.subtract).then_inc(sim_low, 1)
                value = held(eng, at(sim_low, b, 3 * j + 1))
                eng.wait_ge(setup_pool, 1)
                eng.wait_ge(sim_low, value)
                eng.tensor_copy(sim_hm[:, j, :, 1, :], rest).then_inc(sim_low, 1)
                value = held(eng, at(sim_low, b, 3 * j + 2))
                eng.wait_ge(setup_pool, 1)
                eng.wait_ge(sim_low, value)
                eng.tensor_tensor(low, rest, sim_hm[:, j, :, 1, :], ALU.subtract).then_inc(sim_low, 1)

            def add_head(b, j, h):
                eng.wait_ge(prob_masked, at(prob_masked, b, j * FH + h + 1))
                if h == 1:
                    if later(b):
                        value = held(eng, at(acc_tp, b, 0))
                        eng.wait_ge(setup_pool, 1)
                        eng.wait_ge(acc_tp, value)
                    left_in = prob[:, j * FH, :]
                else:
                    value = held(eng, at(acc_added, b, j * (FH - 1) + h - 1))
                    eng.wait_ge(setup_pool, 1)
                    eng.wait_ge(acc_added, value)
                    left_in = acc[:, j, :]
                eng.tensor_tensor(acc[:, j, :], left_in, prob[:, j * FH + h, :], ALU.add).then_inc(acc_added, 1)

            def prologue():
                eng.memset(half_neg[:, :], -0.5).then_inc(setup_pool, 1)
                eng.memset(v_ones[:, :, :], 1.0).then_inc(setup_pool, 1)
                eng.wait_ge(setup_pool, 2)
                rstd(0)
                qk_pieces(0)
                copy_v(0)
                rstd(1)
                qk_pieces(1)
                scale(0)
                sim_pieces(0, 0)
                sim_pieces(0, 1)

            def iteration(i, d, f, a, p):
                if a:
                    copy_v(i + 1)
                if f:
                    copy_x2(i)
                if p:
                    rstd(i + 2)
                if f:
                    add_head(i, 0, 1)
                    add_head(i, 0, 2)
                if p:
                    qk_pieces(i + 2)
                if f:
                    for h in range(3, FH):
                        add_head(i, 0, h)
                if f:
                    add_head(i, 1, 1)
                    add_head(i, 1, 2)
                if a:
                    scale(i + 1)
                if f:
                    add_head(i, 1, 3)
                if a:
                    sim_pieces(i + 1, 0)
                    sim_pieces(i + 1, 1)
                if f:
                    for h in range(4, FH):
                        add_head(i, 1, h)

            schedule(eng, prologue, iteration)

        @block.scalar
        def _(eng):
            def xhat_back(b):
                eng.wait_ge(xhat_tp, every(xhat_tp, b))
                if later(b):
                    eng.wait_ge(v_made, at(v_made, b, 0))
                eng.activation(xhat_t[:, :], misc[0][:, 0:T], ACT.Copy).then_inc(xhat_t_made, 1)

            def qk_high_piece(b):
                eng.wait_ge(qk_made, every(qk_made, b))
                if later(b):
                    eng.wait_ge(stack_in, at(stack_in, b, 0))
                eng.activation(qk_piece[:, 0, :], misc[1][:, :], ACT.Copy).then_inc(qk_high, 1)

            def v_back(b):
                eng.wait_ge(v_made, every(v_made, b))
                if later(b):
                    eng.wait_ge(v_copied, at(v_copied, b, 0))
                eng.activation(v_next[:, :, :], misc[0][:, 0:TILES * HD].rearrange("p (j e) -> p j e", e=HD), ACT.Copy).then_inc(v_next_made, 1)

            def max_back(b):
                eng.wait_ge(max_tp, every(max_tp, b))
                if later(b):
                    eng.wait_ge(max_row_in, at(max_row_in, b, 0))
                eng.activation(max_t[:, :], misc[1][0:H * TILES, 0:P], ACT.Copy).then_inc(max_t_made, 1)

            def att_exp(b, u):
                if u == 0:
                    if later(b):
                        eng.wait_ge(av_made, at(av_made, b, 0))
                eng.wait_ge(att_scores, at(att_scores, b, u + 1))
                if u < 8:
                    dst = probs0[:, 2 * u:2 * u + 2, :].rearrange("p h t -> p (h t)")
                else:
                    dst = probs1[:, 4 * (u - 8):4 * (u - 7), :].rearrange("p h t -> p (h t)")
                eng.activation(dst, att[u % 2][:, :], ACT.Exp, scale=float(HD) ** -0.5).then_inc(att_probs, 1)

            def y_back(b):
                eng.wait_ge(y_tp, every(y_tp, b))
                if later(b):
                    eng.wait_ge(proj_made, at(proj_made, b, 0))
                eng.activation(y_t[:, :], misc[0][:, 0:T], ACT.Copy).then_inc(y_t_made, 1)

            def xn_back(b):
                eng.wait_ge(xn_tp, every(xn_tp, b))
                if later(b):
                    eng.wait_ge(hidden, at(hidden, b, 0))
                if later(b):
                    eng.wait_ge(sim_made, at(sim_made, b, 0))
                eng.activation(xn_t[:, :], misc[1][:, 0:T], ACT.Copy).then_inc(xn_t_made, 1)

            def sim_back(b, j):
                eng.wait_ge(sim_made, at(sim_made, b, j + 1))
                if later(b):
                    eng.wait_ge(select_step, at(select_step, b, 0))
                if later(b):
                    eng.wait_ge(sim_low, at(sim_low, b, 0))
                eng.activation(sim[:, j, :], misc[j][:, :], ACT.Copy).then_inc(sim_kept, 1)
                eng.wait_ge(sim_kept, at(sim_kept, b, j + 1))
                if later(b):
                    eng.wait_ge(piece_tp, at(piece_tp, b, 0))
                v = sim[:, j, :].rearrange("p (h k) -> p h k", h=FH)
                eng.activation(sim_hm[:, j, :, 0, :], v, ACT.Copy).then_inc(sim_high, 1)

            def pieces_back(b, n):
                eng.wait_ge(piece_tp, at(piece_tp, b, n + 1))
                if later(b):
                    eng.wait_ge(scores_made, at(scores_made, b, 0))
                j = n // 2
                if n % 2 == 0:
                    eng.activation(hm_t[:, j, :, :].rearrange("p h t -> p (h t)"), misc[0][:, :].bitcast(BF16), ACT.Copy).then_inc(piece_t_made, 1)
                else:
                    eng.activation(lo_t[:, j, :, :].rearrange("p h t -> p (h t)"),
                                   misc[1][:, 0:BANK // 2].bitcast(BF16), ACT.Copy).then_inc(piece_t_made, 1)

            def activate(b, n):
                eng.wait_ge(hidden, at(hidden, b, n + 1))
                if later(b):
                    eng.wait_ge(gated, at(gated, b, 0))
                eng.activation(act_t[:, 2 * n:2 * n + 2, :].rearrange("p c t -> p (c t)"),
                               misc[(n + 1) % 2][:, :], ACT.Gelu).then_inc(act_made, 1)

            def best_exp(b, j):
                eng.wait_ge(shifted_made, at(shifted_made, b, j + 1))
                eng.activation(exps[:, j, :, :].rearrange("p h k -> p (h k)"),
                               shifted[:, j, :, :].rearrange("p h k -> p (h k)"), ACT.Exp).then_inc(exps_made, 1)

            def log_sum(b, j):
                eng.wait_ge(total_made, at(total_made, b, j + 1))
                eng.activation(log_total[:, j, :], total[:, j, :], ACT.Ln).then_inc(log_made, 1)

            def threshold(b, j):
                eng.wait_ge(cut_arg_made, at(cut_arg_made, b, j + 1))
                eng.activation(cut_prob[:, j, :], cut_arg[:, j, :], ACT.Exp).then_inc(cut_prob_made, 1)

            def pair_probs(b, j, h):
                g = j * FH + h
                eng.wait_ge(scores_made, at(scores_made, b, g + 1))
                if later(b):
                    eng.wait_ge(acc_added, at(acc_added, b - 1, j * (FH - 1) + max(h, 1)))
                elif g == 0:
                    eng.wait_ge(setup_dve, 1)
                eng.activation(prob[:, g, :], score[g % 2][:, :], ACT.Exp,
                               bias=neg_lse[:, j, h:h + 1]).then_inc(prob_made, 1)

            def prologue():
                xhat_back(0)
                qk_high_piece(0)
                v_back(0)
                max_back(0)
                for u in range(MAX_STEPS):
                    att_exp(0, u)
                xhat_back(1)
                qk_high_piece(1)
                v_back(1)
                y_back(0)
                xn_back(0)
                sim_back(0, 0)
                sim_back(0, 1)

            def iteration(i, d, f, a, p):
                if f:
                    for n in range(4):
                        pieces_back(i, n)
                    best_exp(i, 0)
                    log_sum(i, 0)
                    threshold(i, 0)
                    for h in range(FH):
                        pair_probs(i, 0, h)
                if a:
                    max_back(i + 1)
                    for u in range(MAX_STEPS):
                        att_exp(i + 1, u)
                if f:
                    for n in range(4):
                        activate(i, n)
                    best_exp(i, 1)
                    log_sum(i, 1)
                    threshold(i, 1)
                if p:
                    xhat_back(i + 2)
                if f:
                    pair_probs(i, 1, 0)
                if p:
                    qk_high_piece(i + 2)
                    v_back(i + 2)
                if f:
                    pair_probs(i, 1, 1)
                    pair_probs(i, 1, 2)
                if a:
                    y_back(i + 1)
                if f:
                    for h in range(3, 6):
                        pair_probs(i, 1, h)
                if a:
                    xn_back(i + 1)
                if f:
                    pair_probs(i, 1, 6)
                    pair_probs(i, 1, 7)
                if a:
                    sim_back(i + 1, 0)
                    sim_back(i + 1, 1)

            schedule(eng, prologue, iteration)

        @block.vector
        def _(eng):

            def ln1(b):
                eng.wait_ge(x_in, every(x_in, b))
                for j in range(TILES):
                    eng.bn_stats(stat1[:, j, :], xin[:, j, :]).then_inc(ln1_step, 1)
                value = held(eng, at(ln1_step, b, TILES))
                eng.wait_ge(setup_dve, 1)
                eng.wait_ge(ln1_step, value)
                for j in range(TILES):
                    eng.bn_aggr(mv1[:, j, :], stat1[:, j, :]).then_inc(ln1_step, 1)
                eng.wait_ge(ln1_step, at(ln1_step, b, 2 * TILES))
                if later(b):
                    eng.wait_ge(rstd1_made, at(rstd1_made, b, 0))
                eng.tensor_scalar(ln_tmp[:, :], mv1[:, :, 1], LN_EPS, None, ALU.add).then_inc(ln1_step, 1)

            def make_xhat(b):
                eng.wait_ge(rstd1_made, every(rstd1_made, b))
                eng.wait_ge(ln1_step, every(ln1_step, b))
                if later(b):
                    eng.wait_ge(xhat_tp, at(xhat_tp, b, 0))
                for j in range(TILES):
                    eng.tensor_scalar(xhat[:, j, :], xin[:, j, :], mv1[:, j, 0:1], rstd1[:, j:j + 1],
                                      ALU.subtract, ALU.mult).then_inc(xhat_made, 1)

            def qk_remainder(b):
                eng.wait_ge(qk_high, every(qk_high, b))
                eng.wait_ge(qk_made, every(qk_made, b))
                if later(b):
                    eng.wait_ge(qk_low, at(qk_low, b, 0))
                eng.tensor_tensor(qk_rest[:, :], misc[1][:, :], qk_piece[:, 0, :],
                                  ALU.subtract).then_inc(qk_rest_made, 1)

            def take_max(b, u):
                eng.wait_ge(max_scores, at(max_scores, b, u + 1))
                if u == 0:
                    if later(b):
                        eng.wait_ge(max_tp, at(max_tp, b, 0))
                if u < 4:
                    dst, src = neg_max[:, 4 * u:4 * u + 4, 0], att[u % 2][:, :].rearrange("p (h k) -> p h k", h=4)
                else:
                    dst = neg_max[:, 2 * (u - 4):2 * (u - 3), 1]
                    src = att[u % 2][:, :].rearrange("p (h k) -> p h k", h=2)
                eng.tensor_reduce(dst, src, AX.X, ALU.max, negate=True).then_inc(max_taken, 1)

            def make_y(b):
                eng.wait_ge(av_made, every(av_made, b))
                eng.reciprocal(recip[:, :, :], av[:, :, :, HD]).then_inc(recip_made, 1)
                eng.wait_ge(recip_made, every(recip_made, b))
                if later(b):
                    eng.wait_ge(y_tp, at(y_tp, b, 0))
                for_all = recip[:, :, :].rearrange("p t h -> p (t h)").unsqueeze(2).broadcast_to([P, TILES * H, HD])
                eng.tensor_tensor(y[:, :, :].rearrange("p t (h e) -> p (t h) e", e=HD),
                                  av[:, :, :, 0:HD].rearrange("p t h e -> p (t h) e"),
                                  for_all, ALU.mult).then_inc(y_made, 1)

            def make_x2(b):
                eng.wait_ge(proj_made, every(proj_made, b))
                eng.wait_ge(xres_in, every(xres_in, b))
                if later(b):
                    eng.wait_ge(x2_copied, at(x2_copied, b, 0))
                if later(b):
                    eng.wait_ge(xn_made, at(xn_made, b, 0))
                eng.tensor_tensor(x2[:, :, :].rearrange("p j d -> p (j d)"),
                                  xres[:, :, :].rearrange("p j d -> p (j d)"),
                                  att[1][:, 0:TILES * D], ALU.add).then_inc(x2_made, 1)
                eng.wait_ge(x2_made, every(x2_made, b))
                if later(b):
                    eng.wait_ge(scale2_made, at(scale2_made, b, 0))
                for j in range(TILES):
                    eng.bn_stats(stat2[:, j, :], x2[:, j, :]).then_inc(ln2_step, 1)
                value = held(eng, at(ln2_step, b, TILES))
                eng.wait_ge(setup_dve, 1)
                eng.wait_ge(ln2_step, value)
                for j in range(TILES):
                    eng.bn_aggr(mv2[:, j, :], stat2[:, j, :]).then_inc(ln2_step, 1)
                eng.wait_ge(ln2_step, at(ln2_step, b, 2 * TILES))
                eng.tensor_scalar(bounded[:, :], mv2[:, :, 1], LN_EPS, 1e-24 / D, ALU.add,
                                  ALU.mult).then_inc(ln2_step, 1)
                eng.wait_ge(ln2_step, at(ln2_step, b, 2 * TILES + 1))
                eng.tensor_tensor(bounded[:, :], mv2[:, :, 1], bounded[:, :], ALU.max).then_inc(ln2_step, 1)

            def make_xn(b):
                eng.wait_ge(scale2_made, every(scale2_made, b))
                eng.wait_ge(ln2_step, every(ln2_step, b))
                if later(b):
                    eng.wait_ge(xn_tp, at(xn_tp, b, 0))
                for j in range(TILES):
                    eng.tensor_scalar(xn[:, j, :], x2[:, j, :], mv2[:, j, 0:1], scale2[:, j:j + 1],
                                      ALU.subtract, ALU.mult).then_inc(xn_made, 1)

            def select(b, j):
                n = j * SELECT
                value = held(eng, at(sim_kept, b, j + 1))
                eng.wait_ge(setup_dve, 1)
                eng.wait_ge(sim_kept, value)
                keys_of = [sim[:, j, l * KEYS:(l + 1) * KEYS] for l in range(LISTS)]
                for l in range(LISTS):
                    eng.max(top[:, l, 0:8], keys_of[l]).then_inc(select_step, 1)
                    n += 1
                value = held(eng, at(select_step, b, n))
                eng.wait_ge(setup_dve, 1)
                eng.wait_ge(select_step, value)
                for l in range(LISTS):
                    eng.match_replace(left[:, l, :], top[:, l, 0:8], keys_of[l], LOWEST).then_inc(select_step, 1)
                    n += 1
                value = held(eng, at(select_step, b, n))
                eng.wait_ge(setup_dve, 1)
                eng.wait_ge(select_step, value)
                for l in range(LISTS):
                    eng.max(top[:, l, 8:16], left[:, l, :]).then_inc(select_step, 1)
                    n += 1
                value = held(eng, at(select_step, b, n))
                eng.wait_ge(setup_dve, 1)
                eng.wait_ge(select_step, value)
                col = 0
                for a0, na, nb in PAIR_BLOCKS:
                    dst = cand[:, :, col:col + na * nb].rearrange("p h (a b) -> p h a b", b=nb)
                    xs = top[:, 0:LISTS:2, a0:a0 + na].unsqueeze(3).broadcast_to([P, FH, na, nb])
                    ys = top[:, 1:LISTS:2, 0:nb].unsqueeze(2).broadcast_to([P, FH, na, nb])
                    eng.tensor_tensor(dst, xs, ys, ALU.add).then_inc(select_step, 1)
                    n += 1
                    col += na * nb
                ends = top[:, :, 0:TOPK:TOPK - 1].rearrange("p (h a) e -> p h a e", a=2)
                eng.tensor_reduce(size[:, j, :], ends, AX.XY, ALU.add, apply_absolute_value=True).then_inc(select_step, 1)
                n += 1
                value = held(eng, at(select_step, b, n))
                eng.wait_ge(setup_dve, 1)
                eng.wait_ge(select_step, value)
                for h in range(FH):
                    eng.max(best[:, j, h, 0:8], cand[:, h, :]).then_inc(select_step, 1)
                    n += 1
                value = held(eng, at(select_step, b, n))
                eng.wait_ge(setup_dve, 1)
                eng.wait_ge(select_step, value)
                for h in range(FH):
                    eng.match_replace(cand_left[:, h, :], best[:, j, h, 0:8], cand[:, h, :], LOWEST).then_inc(select_step, 1)
                    n += 1
                value = held(eng, at(select_step, b, n))
                eng.wait_ge(setup_dve, 1)
                eng.wait_ge(select_step, value)
                for h in range(FH):
                    eng.max(best[:, j, h, 8:16], cand_left[:, h, :]).then_inc(select_step, 1)
                    n += 1
                value = held(eng, at(select_step, b, n))
                eng.wait_ge(setup_dve, 1)
                eng.wait_ge(select_step, value)
                eng.scalar_tensor_tensor(cut[:, j, :], size[:, j, :], -float(2 ** -22), best[:, j, :, TOPK - 1],
                                         ALU.mult, ALU.add).then_inc(select_step, 1)
                n += 1
                eng.tensor_tensor(shifted[:, j, :, :], best[:, j, :, :],
                                  best[:, j, :, 0:1].broadcast_to([P, FH, TOPK]),
                                  ALU.subtract).then_inc(shifted_made, 1)

            def sum_best(b, j):
                eng.wait_ge(exps_made, at(exps_made, b, j + 1))
                eng.tensor_reduce(total[:, j, :], exps[:, j, :, :], AX.X, ALU.add).then_inc(total_made, 1)

            def log_sum_exp(b, j):
                eng.wait_ge(log_made, at(log_made, b, j + 1))
                if j == 0:
                    if later(b):
                        eng.wait_ge(prob_made, at(prob_made, b, 0))
                eng.scalar_tensor_tensor(neg_lse[:, j, :], log_total[:, j, :], -1.0, best[:, j, :, 0],
                                         ALU.mult, ALU.subtract).then_inc(lse_step, 1)
                eng.wait_ge(lse_step, at(lse_step, b, j + 1))
                eng.wait_ge(select_step, at(select_step, b, (j + 1) * SELECT))
                eng.tensor_tensor(cut_arg[:, j, :], cut[:, j, :], neg_lse[:, j, :], ALU.add).then_inc(cut_arg_made, 1)

            def mask(b, j, h):
                g = j * FH + h
                if h == 0:
                    eng.wait_ge(cut_prob_made, at(cut_prob_made, b, j + 1))
                eng.wait_ge(prob_made, at(prob_made, b, g + 1))
                eng.scalar_tensor_tensor(prob[:, g, :], prob[:, g, :], cut_prob[:, j, h:h + 1], prob[:, g, :],
                                         ALU.is_ge, ALU.mult).then_inc(prob_masked, 1)

            def gate(b):
                eng.wait_ge(act_made, every(act_made, b))
                if later(b):
                    eng.wait_ge(down_made, at(down_made, b, 0))
                for n in range(4):
                    j, half = n // 2, n % 2
                    eng.wait_ge(acc_tp, at(acc_tp, b, n + 1))
                    chunks, toks = slice(4 * half, 4 * half + 4), slice(j * P, (j + 1) * P)
                    eng.tensor_tensor(gated_t[:, chunks, toks],
                                      misc[half][:, :].rearrange("p (c t) -> p c t", t=P),
                                      act_t[:, chunks, toks], ALU.mult).then_inc(gated, 1)

            def finish(b):
                eng.wait_ge(down_made, every(down_made, b))
                eng.wait_ge(x2_copied, every(x2_copied, b))
                if later(b):
                    eng.wait_ge(out_stored, at(out_stored, b, 0))
                eng.tensor_tensor(fin[:, :, :].rearrange("p j d -> p (j d)"),
                                  x2_kept[:, :, :].rearrange("p j d -> p (j d)"),
                                  misc[0][:, 0:TILES * D], ALU.add).then_inc(fin_made, 1)

            def prologue():
                eng.wait_ge(consts_in, 32)
                eng.tensor_copy(cb[:, :], consts_f).then_inc(setup_dve, 1)
                eng.wait_ge(weights_in, 7 * 16)
                eng.tensor_scalar(wdt[:, :], wdt[:, :], gam[:, 0:1], None, ALU.mult).then_inc(setup_done, 1)
                eng.wait_ge(wkey_made, 1)
                eng.tensor_scalar(wkey[:, :], misc[0][:, :], gam[:, 0:1], None, ALU.mult).then_inc(setup_done, 1)
                ln1(0)
                make_xhat(0)
                qk_remainder(0)
                for u in range(MAX_STEPS):
                    take_max(0, u)
                ln1(1)
                make_xhat(1)
                qk_remainder(1)
                make_y(0)
                make_x2(0)
                make_xn(0)

            def iteration(i, d, f, a, p):
                if f:
                    select(i, 0)
                if a:
                    for u in range(0, 3):
                        take_max(i + 1, u)
                if f:
                    sum_best(i, 0)
                if a:
                    for u in range(3, 6):
                        take_max(i + 1, u)
                if f:
                    log_sum_exp(i, 0)
                if a:
                    for u in range(6, MAX_STEPS):
                        take_max(i + 1, u)
                if d:
                    gate(i - 1)
                if f:
                    select(i, 1)
                if d:
                    finish(i - 1)
                if p:
                    ln1(i + 2)
                if f:
                    mask(i, 0, 0)
                    sum_best(i, 1)
                    mask(i, 0, 1)
                    log_sum_exp(i, 1)
                if p:
                    make_xhat(i + 2)
                if f:
                    mask(i, 0, 2)
                    mask(i, 0, 3)
                if p:
                    qk_remainder(i + 2)
                if f:
                    for h in range(4, FH):
                        mask(i, 0, h)
                if a:
                    make_y(i + 1)
                if f:
                    mask(i, 1, 0)
                    mask(i, 1, 1)
                if a:
                    make_x2(i + 1)
                if f:
                    mask(i, 1, 2)
                    mask(i, 1, 3)
                if a:
                    make_xn(i + 1)
                if f:
                    for h in range(4, FH):
                        mask(i, 1, h)

            schedule(eng, prologue, iteration)

        @block.tensor
        def _(eng):
            def fold_keys():
                eng.wait_ge(weights_in, 7 * 16)
                for l in range(LISTS):
                    ins = eng.matmul(misc[0][:, l * KEYS:(l + 1) * KEYS], wqs[:, l, :],
                                     keyt[:, l * KEYS:(l + 1) * KEYS], start=True, stop=True)
                ins.then_inc(wkey_made, 1)

            def two_transposes(bank, src, sig):
                for j in range(TILES):
                    ins = eng.transpose(bank[:, j * P:(j + 1) * P], src[:, j, :], ident[:, :])
                ins.then_inc(sig, 1)

            def xhat_transpose(b, reader, of_batch):
                eng.wait_ge(xhat_made, every(xhat_made, b))
                eng.wait_ge(reader, every(reader, of_batch))
                two_transposes(misc[0], xhat, xhat_tp)

            def project_qkv(b, reader=None, of_batch=None):
                eng.wait_ge(xhat_t_made, every(xhat_t_made, b))
                if reader:
                    eng.wait_ge(reader, every(reader, of_batch))
                eng.matmul(misc[1][:, 0:T], wa[:, 0:D], xhat_t[:, :], start=True, stop=True)
                eng.matmul(misc[1][:, T:2 * T], wa[:, 2 * HD:D + 2 * HD], xhat_t[:, :],
                           start=True, stop=True).then_inc(qk_made, 1)
                for j in range(TILES):
                    ins = eng.matmul(misc[0][:, j * HD:(j + 1) * HD], xhat_t[:, j * P:(j + 1) * P],
                                     wa[:, D + HD:D + 2 * HD], start=True, stop=True)
                ins.then_inc(v_made, 1)

            def scores_for_max(b, u):
                if u == 0:
                    eng.wait_ge(stack_in, every(stack_in, b))
                    if later(b):
                        eng.wait_ge(y_made, at(y_made, b, 0))
                elif u == 1:
                    if later(b):
                        eng.wait_ge(x2_made, at(x2_made, b, 0))
                else:
                    eng.wait_ge(max_taken, at(max_taken, b, u - 1))
                bank = att[u % 2]
                nh, nk, h0, j = (4, P, 4 * u, 0) if u < 4 else (2, T, 2 * (u - 4), 1)
                eng.matmul(bank[:, :], ident_bf, mask_q0 if j == 0 else mask_q1, start=True, stop=False)
                for n in range(nh):
                    ins = eng.matmul(bank[:, n * nk:(n + 1) * nk], q_stack[0:STACK, h0 + n, j * P:(j + 1) * P],
                                     k_stack[0:STACK, 0:nk], start=False, stop=n == nh - 1)
                ins.then_inc(max_scores, 1)

            def max_transpose(b):
                eng.wait_ge(max_taken, every(max_taken, b))
                if not later(b):
                    eng.wait_ge(qk_rest_made, every(qk_rest_made, b))
                else:
                    eng.wait_ge(piece_t_made, every(piece_t_made, b - 1))
                eng.transpose(misc[1][0:H * TILES, 0:P], neg_max[:, :, :].rearrange("p h j -> p (h j)"),
                              ident[:, :]).then_inc(max_tp, 1)

            def scores_for_probs(b, u):
                if u == 0:
                    eng.wait_ge(max_row_in, every(max_row_in, b))
                    if not later(b):
                        eng.wait_ge(ones_in, 16)
                if u < 2:
                    eng.wait_ge(max_taken, every(max_taken, b))
                else:
                    eng.wait_ge(att_probs, at(att_probs, b, u - 1))
                bank = att[u % 2]
                if u < 8:
                    m, k, q = mask_t0, k_stack[:, 0:P], q_stack[:, 2 * u:2 * u + 2, :]
                else:
                    m, k, q = mask_t1, k_stack[:, P:T], q_stack[:, 4 * (u - 8):4 * (u - 7), P:T]
                eng.matmul(bank[:, :], ident_bf, m, start=True, stop=False)
                eng.matmul(bank[:, :], k, q, start=False, stop=True).then_inc(att_scores, 1)

            def weigh_values(b):
                eng.wait_ge(att_probs, every(att_probs, b))
                eng.wait_ge(v_copied, every(v_copied, b))
                for h in range(H):
                    eng.matmul(av[:, 0, h, :], probs0[:, h, 0:P], v_ones[:, 0, :], start=True, stop=True)
                    eng.matmul(av[:, 1, h, :], probs0[:, h, P:T], v_ones[:, 0, :], start=True, stop=False)
                    ins = eng.matmul(av[:, 1, h, :], probs1[:, h, :], v_ones[:, 1, :], start=False, stop=True)
                ins.then_inc(av_made, 1)

            def y_transpose(b, reader, of_batch):
                eng.wait_ge(y_made, every(y_made, b))
                eng.wait_ge(reader, every(reader, of_batch))
                two_transposes(misc[0], y, y_tp)

            def project_y(b):
                eng.wait_ge(y_t_made, every(y_t_made, b))
                for j in range(TILES):
                    ins = eng.matmul(att[1][:, j * D:(j + 1) * D], y_t[:, j * P:(j + 1) * P], wp[:, :],
                                     start=True, stop=True)
                ins.then_inc(proj_made, 1)

            def xn_transpose(b, reader, of_batch):
                eng.wait_ge(xn_made, every(xn_made, b))
                eng.wait_ge(reader, every(reader, of_batch))
                two_transposes(misc[1], xn, xn_tp)

            def key_scores(b):
                eng.wait_ge(xn_t_made, every(xn_t_made, b))
                eng.wait_ge(y_t_made, every(y_t_made, b))
                for j in range(TILES):
                    eng.matmul(misc[j][:, :], xn_t[:, j * P:(j + 1) * P], wkey[:, :],
                               start=True, stop=True).then_inc(sim_made, 1)

            def hidden_chunks(b, n, reader):
                if n < 2:
                    eng.wait_ge(reader[0], every(*reader))
                else:
                    eng.wait_ge(act_made, at(act_made, b, n - 1))
                bank = misc[(n + 1) % 2]
                for c in (2 * n, 2 * n + 1):
                    ins = eng.matmul(bank[:, (c % 2) * T:(c % 2 + 1) * T], wdt[:, c * P:(c + 1) * P],
                                     xn_t[:, :], start=True, stop=True)
                ins.then_inc(hidden, 1)

            def piece_transposes(b, j):
                eng.wait_ge(sim_low, at(sim_low, b, 3 * (j + 1)))
                eng.wait_ge(sim_high, at(sim_high, b, j + 1))
                if j == 0:
                    eng.wait_ge(sim_kept, every(sim_kept, b))
                else:
                    eng.wait_ge(piece_t_made, at(piece_t_made, b, 1))
                dst = misc[0][:, :].bitcast(BF16)
                for h in range(FH):
                    ins = eng.transpose(dst[:, h * P:(h + 1) * P],
                                        sim_hm[:, j, h, :, :].rearrange("p s k -> p (s k)"), ident_bf)
                ins.then_inc(piece_tp, 1)
                if j:
                    eng.wait_ge(piece_t_made, at(piece_t_made, b, 2))
                dst = misc[1][:, 0:BANK // 2].bitcast(BF16)
                for n in range(FH // 2):
                    ins = eng.transpose(dst[:, n * P:(n + 1) * P], sim_lo[:, j, n * P:(n + 1) * P], ident_bf)
                ins.then_inc(piece_tp, 1)

            def pair_scores(b, j, h):
                g = j * FH + h
                if h == 0:
                    eng.wait_ge(piece_t_made, at(piece_t_made, b, 2 * j + 2))
                if g >= 2 or later(b):
                    eng.wait_ge(prob_made, at(prob_made, b, g - 1))
                for half in range(2):
                    cols = slice(half * BANK, (half + 1) * BANK)
                    eng.matmul(score[g % 2][:, cols], hm_t[:, j, h, :], sel_high[:, cols], start=True, stop=False)
                    ins = eng.matmul(score[g % 2][:, cols], lo_t[:, j, h // 2, :], sel_low[h % 2][:, cols],
                                     start=False, stop=True)
                ins.then_inc(scores_made, 1)

            def acc_transposes(b, readers):
                for n in range(4):
                    j, half = n // 2, n % 2
                    eng.wait_ge(acc_added, at(acc_added, b, (FH - 1) * (j + 1)))
                    if n < 2:
                        eng.wait_ge(readers[n][0], every(*readers[n]))
                    else:
                        eng.wait_ge(gated, at(gated, b, n - 1))
                    for c in range(4):
                        chunk = 4 * half + c
                        ins = eng.transpose(misc[half][:, c * P:(c + 1) * P], acc[:, j, chunk * P:(chunk + 1) * P],
                                            ident[:, :])
                    ins.then_inc(acc_tp, 1)

            def expert_output(b):
                eng.wait_ge(gated, every(gated, b))
                for j in range(TILES):
                    for c in range(CH):
                        ins = eng.matmul(misc[0][:, j * D:(j + 1) * D], gated_t[:, c, j * P:(j + 1) * P],
                                         wu[:, c, :], start=c == 0, stop=c == CH - 1)
                ins.then_inc(down_made, 1)

            def prologue():
                fold_keys()
                xhat_transpose(0, setup_done, 0)
                project_qkv(0)
                for u in range(MAX_STEPS):
                    scores_for_max(0, u)
                max_transpose(0)
                for u in range(MAX_STEPS):
                    scores_for_probs(0, u)
                weigh_values(0)
                xhat_transpose(1, v_next_made, 0)
                project_qkv(1, max_t_made, 0)
                y_transpose(0, v_next_made, 1)
                project_y(0)
                eng.wait_ge(setup_done, 2)
                xn_transpose(0, qk_rest_made, 1)
                key_scores(0)

            def iteration(i, d, f, a, p):
                if f:
                    piece_transposes(i, 0)
                    piece_transposes(i, 1)
                    pair_scores(i, 0, 0)
                    pair_scores(i, 0, 1)
                if a:
                    for u in range(0, 7):
                        scores_for_max(i + 1, u)
                for h in range(2, FH):
                    if f:
                        pair_scores(i, 0, h)
                    if a and h + 5 < MAX_STEPS:
                        scores_for_max(i + 1, h + 5)
                readers = [(piece_t_made, i) if f else (act_made, i - 1)] * 2
                if a:
                    max_transpose(i + 1)
                    readers[1] = (max_t_made, i + 1)
                if d:
                    acc_transposes(i - 1, readers)
                    expert_output(i - 1)
                    readers = [(fin_made, i - 1), (gated, i - 1)]
                if a:
                    for u in range(MAX_STEPS):
                        scores_for_probs(i + 1, u)
                if f:
                    for n in range(4):
                        hidden_chunks(i, n, readers[(n + 1) % 2])
                    readers = [(act_made, i)] * 2
                    pair_scores(i, 1, 0)
                    pair_scores(i, 1, 1)
                if a:
                    weigh_values(i + 1)
                if p:
                    xhat_transpose(i + 2, *readers[0])
                    project_qkv(i + 2, *readers[1])
                    readers = [(v_next_made, i + 2), (qk_rest_made, i + 2)]
                if f:
                    pair_scores(i, 1, 2)
                if a:
                    y_transpose(i + 1, *readers[0])
                if f:
                    pair_scores(i, 1, 3)
                if a:
                    project_y(i + 1)
                if f:
                    pair_scores(i, 1, 4)
                    pair_scores(i, 1, 5)
                if a:
                    xn_transpose(i + 1, *readers[1])
                if f:
                    pair_scores(i, 1, 6)
                    pair_scores(i, 1, 7)
                if a:
                    key_scores(i + 1)

            schedule(eng, prologue, iteration)


def constants():
    import numpy as np
    eye = np.eye(P, dtype=np.float32)
    q, k = np.arange(P)[:, None], np.arange(P)[None, :]
    tri = np.where(k > q, np.float32(MASKED), np.float32(0))
    none = np.zeros((P, P), np.float32)
    masks = [np.tile(tri, (1, 4)), np.tile(np.hstack([none, tri]), (1, 2)),
             np.tile(np.hstack([tri.T, none]), (1, 2)), np.tile(tri.T, (1, 4))]
    pair = np.arange(EXPERTS)
    spread = np.concatenate([(np.arange(KEYS)[:, None] == pair // KEYS),
                             (np.arange(KEYS)[:, None] == pair % KEYS)]).astype(np.float32)
    zero = np.zeros_like(spread)
    sel = [np.vstack([spread, spread]), np.vstack([spread, zero]), np.vstack([zero, spread])]
    return np.ascontiguousarray(np.hstack([eye] + masks + sel + [np.ones((P, T), np.float32)]))


def kernel(L0_attn_x, L0_attn_w_attn, L0_attn_w_proj, L0_ffn_gamma, L0_ffn_wq, L0_ffn_keys,
           L0_ffn_table_down, L0_ffn_table_up):
    import numpy as np
    import concourse.bacc as bacc
    from concourse.bass_utils import run_bass_kernel_spmd

    arrays = {
        "x": np.asarray(L0_attn_x),
        "w_attn": np.asarray(L0_attn_w_attn),
        "w_proj": np.asarray(L0_attn_w_proj),
        "gamma": np.asarray(L0_ffn_gamma).reshape(D, 1),
        "wq": np.asarray(L0_ffn_wq).reshape(2, FH, DK, D).transpose(2, 1, 0, 3).reshape(DK, LISTS, D),
        "keys": np.asarray(L0_ffn_keys).transpose(3, 0, 2, 1).reshape(DK, LISTS * KEYS),
        "down": np.asarray(L0_ffn_table_down)[:EXPERTS].T,
        "up": np.asarray(L0_ffn_table_up)[:EXPERTS],
        "consts": constants(),
    }
    arrays = {n: np.ascontiguousarray(a) for n, a in arrays.items()}
    nc = bacc.Bacc("TRN2", target_bir_lowering=False, num_devices=1)
    args = [nc.dram_tensor(n, a.shape, mybir.dt.from_np(a.dtype), kind="ExternalInput").ap()
            for n, a in arrays.items()]
    out = nc.dram_tensor("out", (BATCHES, T, D), FP32, kind="ExternalOutput").ap()
    build(nc, *args, out)
    result = run_bass_kernel_spmd(nc, [arrays], core_ids=[0])
    return result.results[0]["out"]
```

```python
import concourse.bass as bass
from concourse import mybir
from contextlib import ExitStack

FP32 = mybir.dt.float32
BF16 = mybir.dt.bfloat16
FP16 = mybir.dt.float16
ALU = mybir.AluOpType
ACT = mybir.ActivationFunctionType
AX = mybir.AxisListType

P = 128
BATCHES, T, D = 16, 256, 128
TILES = T // P
H, HD = 16, 8
FH, KEYS, DK = 8, 32, 64
EXPERTS = KEYS * KEYS
CH = EXPERTS // P
TOPK = 16
LISTS = 2 * FH
LN_EPS = 1e-5
MASKED = -float(2 ** 100)
LOWEST = -3.0e38
SIM_PEAK = float(2 ** 12)
Q_PIECE = (0, 0, 0, 1, 1, 2)
K_PIECE = (0, 1, 2, 0, 1, 0)
STACK = len(Q_PIECE) * HD
PAIR_BLOCKS = ((0, 1, 16), (1, 1, 8), (2, 2, 5), (4, 4, 3), (8, 8, 1))
PAIRS = sum(na * nb for _, na, nb in PAIR_BLOCKS)
BANK = 512
MAX_STEPS = 12


def later(batch):
    return not isinstance(batch, int) or batch > 0


def held(eng, value):
    return value if isinstance(value, int) else eng.to_reg(value)


def build(nc, x, w_attn, w_proj, gamma, wq, keys, down, up, consts, out):
    ctx = ExitStack()
    with ctx:
        def sb(name, shape, dt=FP32):
            return ctx.enter_context(nc.sbuf_tensor(name, shape, dt))

        raised = {}

        def signal(name, per_batch=1):
            sem = ctx.enter_context(nc.semaphore(name))
            raised[sem] = per_batch
            return sem

        def at(sem, batch, n):
            return batch * raised[sem] + n

        def every(sem, batch):
            return at(sem, batch, raised[sem])

        y_scratch = nc.dram_tensor("y_scratch", (2 * HD, H, T), FP32, kind="Internal").ap()
        q_scratch = nc.dram_tensor("q_scratch", (P, 3, T), BF16, kind="Internal").ap()

        SEL = P + 4 * BANK + T
        ident = sb("ident", [P, P])
        cb = sb("cb", [P, SEL], BF16)
        ident_bf = cb[:, 0:P]
        mask_q0 = cb[:, P:P + BANK]
        mask_q1 = cb[:, P + BANK:P + 2 * BANK]
        mask_t0 = cb[:, P + 2 * BANK:P + 3 * BANK]
        mask_t1 = cb[:, P + 3 * BANK:P + 4 * BANK]
        ones_row = cb[0:1, P + 4 * BANK:SEL]
        ident_h = sb("ident_h", [P, P], FP16)
        sel = sb("sel", [P, EXPERTS], FP16)
        wa = sb("wa", [P, D + 2 * HD])
        wp = sb("wp", [P, D])
        gam = sb("gam", [P, 1])
        wqs = sb("wqs", [DK, LISTS, D])
        keyt = sb("keyt", [DK, LISTS * KEYS])
        wkey = sb("wkey", [P, LISTS * KEYS])
        wdt = sb("wdt", [P, EXPERTS])
        wu = sb("wu", [P, CH, D])

        xin = sb("xin", [P, TILES, D])
        stat1 = sb("stat1", [P, TILES, 6])
        mv1 = sb("mv1", [P, TILES, 2])
        rstd1 = sb("rstd1", [P, TILES])
        half_neg = sb("half_neg", [P, TILES])
        ln_tmp = sb("ln_tmp", [P, TILES])
        xhat = sb("xhat", [P, TILES, D])
        xhat_t = sb("xhat_t", [P, T])
        qk_piece = sb("qk_piece", [P, 3, 2 * T], BF16)
        qk_rest = sb("qk_rest", [P, 2 * T])
        v_next = sb("v_next", [P, TILES, HD])
        q_stack = sb("q_stack", [STACK + 1, H, T], BF16)
        k_stack = sb("k_stack", [STACK + 1, T], BF16)
        v_cols = sb("v_cols", [P, TILES, 32])
        neg_max = sb("neg_max", [P, H, TILES])
        max_t = sb("max_t", [H * TILES, P], BF16)
        probs0 = sb("probs0", [P, H, T])
        probs1 = sb("probs1", [P, H, P])
        weighed = sb("weighed", [P, 2, BANK])
        y_in = sb("y_in", [P, 2, T])
        recip = sb("recip", [P, T])
        y_t = sb("y_t", [P, T])
        xres = sb("xres", [P, TILES, D])
        x2 = sb("x2", [P, TILES, D])
        x2_kept = sb("x2_kept", [P, TILES, D])
        stat2 = sb("stat2", [P, TILES, 6])
        mv2 = sb("mv2", [P, TILES, 2])
        bounded = sb("bounded", [P, TILES])
        scale2 = sb("scale2", [P, TILES])
        xn = sb("xn", [P, TILES, D])
        xn_t = sb("xn_t", [P, T])
        sim = sb("sim", [P, TILES, LISTS * KEYS])
        peak = sb("peak", [P, TILES])
        unit_next = sb("unit_next", [P, TILES])
        unit_inv = sb("unit_inv", [P, TILES])
        unit = sb("unit", [P, TILES])
        neg_unit = sb("neg_unit", [P, TILES])
        pieces = sb("pieces", [P, TILES, FH, 2, 2 * KEYS], FP16)
        pieces_t = sb("pieces_t", [P, TILES, FH, P], FP16)
        top = sb("top", [P, LISTS, TOPK])
        left = sb("left", [P, LISTS, KEYS])
        cand = sb("cand", [P, FH, PAIRS])
        cand_left = sb("cand_left", [P, FH, PAIRS])
        best = sb("best", [P, TILES, FH, TOPK])
        size = sb("size", [P, TILES, FH])
        cut = sb("cut", [P, TILES, FH])
        shifted = sb("shifted", [P, TILES, FH, TOPK])
        exps = sb("exps", [P, TILES, FH, TOPK])
        total = sb("total", [P, TILES, FH])
        log_total = sb("log_total", [P, TILES, FH])
        neg_lse = sb("neg_lse", [P, TILES, FH])
        cut_arg = sb("cut_arg", [P, TILES, FH])
        cut_prob = sb("cut_prob", [P, TILES, FH])
        prob = sb("prob", [P, TILES * FH, EXPERTS])
        acc = sb("acc", [P, TILES, EXPERTS])
        act_t = sb("act_t", [P, CH, T])
        gated_t = sb("gated_t", [P, CH, T])
        fin = sb("fin", [P, TILES, D])
        consts_f = prob[:, :, :].rearrange("p a b -> p (a b)")[:, 0:SEL + EXPERTS]

        score = [ctx.enter_context(nc.psum_tensor(f"score{n}", [P, EXPERTS], FP32)) for n in range(2)]
        att = [ctx.enter_context(nc.psum_tensor(f"att{n}", [P, BANK], FP32)) for n in range(2)]
        misc = [ctx.enter_context(nc.psum_tensor(f"misc{n}", [P, BANK], FP32)) for n in range(2)]

        weights_in = signal("weights_in")
        consts_in = signal("consts_in")
        ones_in = signal("ones_in")
        setup_pool = signal("setup_pool", 3)
        setup_dve = signal("setup_dve")
        wkey_made = signal("wkey_made")
        setup_done = signal("setup_done", 2)
        x_in = signal("x_in", 16)
        ln1_step = signal("ln1_step", 5)
        rstd1_made = signal("rstd1_made")
        xhat_made = signal("xhat_made", 2)
        xhat_tp = signal("xhat_tp")
        xhat_t_made = signal("xhat_t_made")
        qk_made = signal("qk_made")
        v_made = signal("v_made")
        qk_high = signal("qk_high")
        qk_rest_made = signal("qk_rest_made")
        qk_middle = signal("qk_middle")
        qk_low = signal("qk_low")
        v_next_made = signal("v_next_made")
        scratch_in = signal("scratch_in", 16)
        stack_in = signal("stack_in", 16 * 2 * len(Q_PIECE))
        max_scores = signal("max_scores", MAX_STEPS)
        max_taken = signal("max_taken", MAX_STEPS)
        max_tp = signal("max_tp")
        max_t_made = signal("max_t_made")
        max_row_in = signal("max_row_in", 16)
        att_scores = signal("att_scores", MAX_STEPS)
        att_probs = signal("att_probs", MAX_STEPS)
        v_copied = signal("v_copied")
        av_made = signal("av_made")
        av_kept = signal("av_kept", 2)
        av_stored = signal("av_stored", 4 * 16)
        y_loaded = signal("y_loaded", 2 * 16)
        recip_made = signal("recip_made")
        y_t_made = signal("y_t_made")
        proj_made = signal("proj_made")
        xres_in = signal("xres_in", 16)
        x2_made = signal("x2_made")
        ln2_step = signal("ln2_step", 6)
        scale2_made = signal("scale2_made")
        xn_made = signal("xn_made", 2)
        xn_tp = signal("xn_tp")
        xn_t_made = signal("xn_t_made")
        sim_made = signal("sim_made", 2)
        sim_kept = signal("sim_kept", 2)
        unit_step = signal("unit_step", 4)
        unit_made = signal("unit_made", 2)
        sim_high = signal("sim_high", 2)
        sim_low = signal("sim_low", 2)
        piece_tp = signal("piece_tp", 2)
        piece_t_made = signal("piece_t_made", 2)
        hidden = signal("hidden", 2)
        act_made = signal("act_made", 2)
        SELECT = 3 * LISTS + len(PAIR_BLOCKS) + 1 + 3 * FH + 1
        select_step = signal("select_step", TILES * SELECT)
        shifted_made = signal("shifted_made", 2)
        exps_made = signal("exps_made", 2)
        total_made = signal("total_made")
        log_made = signal("log_made")
        lse_step = signal("lse_step", 2)
        cut_arg_made = signal("cut_arg_made", 2)
        cut_prob_made = signal("cut_prob_made")
        scores_made = signal("scores_made", TILES * FH)
        prob_made = signal("prob_made", TILES * FH)
        prob_masked = signal("prob_masked", TILES * FH)
        acc_added = signal("acc_added", TILES * (FH - 1))
        x2_copied = signal("x2_copied")
        acc_tp = signal("acc_tp", 2)
        gated = signal("gated", 2)
        down_made = signal("down_made")
        fin_made = signal("fin_made")
        out_stored = signal("out_stored", 16)

        block = ctx.enter_context(nc.Block())

        def schedule(eng, prologue, iteration):
            prologue()
            iteration(0, d=False, f=True, a=True, p=True)
            with eng.Fori(1, BATCHES - 2) as i:
                iteration(i, d=True, f=True, a=True, p=True)
            iteration(BATCHES - 2, d=True, f=True, a=True, p=False)
            iteration(BATCHES - 1, d=True, f=True, a=False, p=False)
            iteration(BATCHES, d=True, f=False, a=False, p=False)

        @block.sync
        def _(eng):
            x_v = x.rearrange("b (j p) d -> b p j d", p=P)
            out_v = out.rearrange("b (j p) d -> b p j d", p=P)

            def load_x(b):
                value = held(eng, at(xhat_made, b, 0))
                if later(b):
                    eng.wait_ge(setup_dve, 1)
                    eng.wait_ge(xhat_made, value)
                eng.dma_start(xin[:, :, :], x_v[b]).then_inc(x_in, 16)

            def load_residual(b):
                value = held(eng, at(x2_made, b, 0))
                if later(b):
                    eng.wait_ge(setup_dve, 1)
                    eng.wait_ge(x2_made, value)
                eng.dma_start(xres[:, :, :], x_v[b]).then_inc(xres_in, 16)

            def stack_pieces(b):
                value = held(eng, every(qk_high, b))
                read = held(eng, at(stack_in, b, 0))
                used = held(eng, at(att_scores, b, 0))
                stored = held(eng, every(scratch_in, b))
                eng.wait_ge(qk_high, value)
                eng.wait_ge(qk_middle, value)
                eng.wait_ge(qk_low, value)
                if later(b):
                    eng.wait_ge(stack_in, read)
                eng.dma_start(q_scratch, qk_piece[:, :, 0:T]).then_inc(scratch_in, 16)
                if later(b):
                    eng.wait_ge(att_scores, used)
                eng.wait_ge(scratch_in, stored)
                view = q_scratch.rearrange("(h d) s t -> s d h t", d=HD)
                for c in range(len(Q_PIECE)):
                    rows = slice(c * HD, (c + 1) * HD)
                    eng.dma_start(q_stack[rows, :, :], view[Q_PIECE[c]]).then_inc(stack_in, 16)
                    eng.dma_start(k_stack[rows, :],
                                  qk_piece[D - 2 * HD:D - HD, K_PIECE[c], T:2 * T]).then_inc(stack_in, 16)

            def place_max_row(b):
                value = held(eng, every(max_t_made, b))
                used = held(eng, at(att_scores, b, 0))
                eng.wait_ge(max_t_made, value)
                if later(b):
                    eng.wait_ge(att_scores, used)
                row = q_stack[STACK:STACK + 1, :, :].rearrange("o h (j t) -> o (h j) t", t=P)
                eng.dma_start(row, max_t[:, :]).then_inc(max_row_in, 16)

            def spread_weighed(b):
                value = held(eng, every(av_kept, b))
                read = held(eng, at(y_loaded, b, 0))
                used = held(eng, at(y_t_made, b, 0))
                stored = held(eng, every(av_stored, b))
                eng.wait_ge(av_kept, value)
                if later(b):
                    eng.wait_ge(y_loaded, read)
                for g in range(4):
                    src = weighed[32 * g:32 * g + 2 * HD, :, :].rearrange("e n (h t) -> e (n h) t", t=T)
                    eng.dma_start(y_scratch[:, 4 * g:4 * g + 4, :], src).then_inc(av_stored, 16)
                if later(b):
                    eng.wait_ge(y_t_made, used)
                eng.wait_ge(av_stored, stored)
                for n in range(2):
                    src = y_scratch[n * HD:(n + 1) * HD, :, :].rearrange("d h t -> h d t")
                    eng.dma_start(y_in[:, n, :], src).then_inc(y_loaded, 16)

            def store(b):
                value = held(eng, every(fin_made, b))
                eng.wait_ge(setup_dve, 1)
                eng.wait_ge(fin_made, value)
                eng.dma_start(out_v[b], fin[:, :, :]).then_inc(out_stored, 16)

            def prologue():
                load_x(0)
                eng.dma_start(consts_f, consts).then_inc(consts_in, 16)
                eng.dma_start(ident[:, :], consts[:, 0:P]).then_inc(consts_in, 16)
                for dst, src in ((wa[:, :], w_attn), (wp[:, :], w_proj), (gam[:, :], gamma),
                                 (wqs[:, :, :], wq), (keyt[:, :], keys), (wdt[:, :], down),
                                 (wu[:, :, :], up.rearrange("(c p) d -> p c d", p=P))):
                    eng.dma_start(dst, src).then_inc(weights_in, 16)
                eng.wait_ge(setup_dve, 3)
                eng.dma_start(k_stack[STACK:STACK + 1, :], ones_row).then_inc(ones_in, 16)
                stack_pieces(0)
                load_x(1)
                load_residual(0)
                place_max_row(0)
                spread_weighed(0)
                stack_pieces(1)

            def iteration(i, d, f, a, p):
                if p:
                    load_x(i + 2)
                if a:
                    load_residual(i + 1)
                    place_max_row(i + 1)
                    spread_weighed(i + 1)
                if d:
                    store(i - 1)
                if p:
                    stack_pieces(i + 2)

            schedule(eng, prologue, iteration)
            eng.wait_ge(out_stored, every(out_stored, BATCHES - 1))

        @block.gpsimd
        def _(eng):
            def rstd(b):
                eng.wait_ge(ln1_step, every(ln1_step, b))
                if later(b):
                    eng.wait_ge(xhat_made, at(xhat_made, b, 0))
                eng.tensor_tensor(rstd1[:, :], ln_tmp[:, :], half_neg[:, :], ALU.pow).then_inc(rstd1_made, 1)

            def qk_low_piece(b):
                eng.wait_ge(qk_middle, every(qk_middle, b))
                if later(b):
                    eng.wait_ge(stack_in, at(stack_in, b, 0))
                    eng.wait_ge(scratch_in, at(scratch_in, b, 0))
                eng.tensor_tensor(qk_piece[:, 2, :], qk_rest[:, :], qk_piece[:, 1, :],
                                  ALU.subtract).then_inc(qk_low, 1)

            def scale(b):
                eng.wait_ge(ln2_step, every(ln2_step, b))
                if later(b):
                    eng.wait_ge(xn_made, at(xn_made, b, 0))
                eng.tensor_tensor(scale2[:, :], bounded[:, :], half_neg[:, :], ALU.pow).then_inc(scale2_made, 1)

            def sim_low_piece(b, j):
                eng.wait_ge(sim_high, at(sim_high, b, j + 1))
                if later(b):
                    eng.wait_ge(piece_tp, at(piece_tp, b, 0))
                v = sim[:, j, :].rearrange("p (h k) -> p h k", h=FH)
                eng.tensor_tensor(pieces[:, j, :, 1, :], v, pieces[:, j, :, 0, :],
                                  ALU.subtract).then_inc(sim_low, 1)

            def add_head(b, j, h):
                eng.wait_ge(prob_masked, at(prob_masked, b, j * FH + h + 1))
                if h == 1:
                    if later(b):
                        eng.wait_ge(acc_tp, at(acc_tp, b, 0))
                    so_far = prob[:, j * FH, :]
                else:
                    eng.wait_ge(acc_added, at(acc_added, b, j * (FH - 1) + h - 1))
                    so_far = acc[:, j, :]
                eng.tensor_tensor(acc[:, j, :], so_far, prob[:, j * FH + h, :], ALU.add).then_inc(acc_added, 1)

            def prologue():
                eng.memset(half_neg[:, :], -0.5).then_inc(setup_pool, 1)
                eng.memset(v_cols[:, :, :], 0.0).then_inc(setup_pool, 1)
                eng.wait_ge(setup_pool, 2)
                eng.memset(v_cols[:, :, HD:2 * HD], 1.0).then_inc(setup_pool, 1)
                rstd(0)
                qk_low_piece(0)
                rstd(1)
                qk_low_piece(1)
                scale(0)
                sim_low_piece(0, 0)
                sim_low_piece(0, 1)

            def iteration(i, d, f, a, p):
                if p:
                    rstd(i + 2)
                if a:
                    scale(i + 1)
                if f:
                    add_head(i, 0, 1)
                    add_head(i, 0, 2)
                if p:
                    qk_low_piece(i + 2)
                if f:
                    add_head(i, 0, 3)
                    add_head(i, 0, 4)
                if a:
                    sim_low_piece(i + 1, 0)
                    sim_low_piece(i + 1, 1)
                if f:
                    for h in range(5, FH):
                        add_head(i, 0, h)
                    for h in range(1, FH):
                        add_head(i, 1, h)

            schedule(eng, prologue, iteration)

        @block.scalar
        def _(eng):
            def xhat_back(b):
                eng.wait_ge(xhat_tp, every(xhat_tp, b))
                if later(b):
                    eng.wait_ge(v_made, at(v_made, b, 0))
                eng.activation(xhat_t[:, :], misc[0][:, 0:T], ACT.Copy).then_inc(xhat_t_made, 1)

            def qk_high_piece(b):
                eng.wait_ge(qk_made, every(qk_made, b))
                if later(b):
                    eng.wait_ge(stack_in, at(stack_in, b, 0))
                    eng.wait_ge(scratch_in, at(scratch_in, b, 0))
                eng.activation(qk_piece[:, 0, :], misc[1][:, :], ACT.Copy).then_inc(qk_high, 1)

            def qk_middle_piece(b):
                eng.wait_ge(qk_rest_made, every(qk_rest_made, b))
                eng.activation(qk_piece[:, 1, :], qk_rest[:, :], ACT.Copy).then_inc(qk_middle, 1)

            def v_back(b):
                eng.wait_ge(v_made, every(v_made, b))
                if later(b):
                    eng.wait_ge(v_copied, at(v_copied, b, 0))
                eng.activation(v_next[:, :, :], misc[0][:, 0:TILES * HD].rearrange("p (j e) -> p j e", e=HD),
                               ACT.Copy).then_inc(v_next_made, 1)

            def copy_v(b):
                if later(b):
                    eng.wait_ge(av_made, at(av_made, b, 0))
                else:
                    eng.wait_ge(setup_pool, 3)
                eng.wait_ge(v_next_made, every(v_next_made, b))
                eng.activation(v_cols[:, :, 0:HD], v_next[:, :, :], ACT.Copy).then_inc(v_copied, 1)

            def max_back(b):
                eng.wait_ge(max_tp, every(max_tp, b))
                if later(b):
                    eng.wait_ge(max_row_in, at(max_row_in, b, 0))
                eng.activation(max_t[:, :], misc[0][0:H * TILES, 0:P], ACT.Copy).then_inc(max_t_made, 1)

            def att_exp(b, u):
                if u == 0 and later(b):
                    eng.wait_ge(av_made, at(av_made, b, 0))
                eng.wait_ge(att_scores, at(att_scores, b, u + 1))
                if u < 8:
                    dst = probs0[:, 2 * u:2 * u + 2, :].rearrange("p h t -> p (h t)")
                else:
                    dst = probs1[:, 4 * (u - 8):4 * (u - 7), :].rearrange("p h t -> p (h t)")
                eng.activation(dst, att[u % 2][:, :], ACT.Exp, scale=float(HD) ** -0.5).then_inc(att_probs, 1)

            def weighed_back(b):
                eng.wait_ge(av_made, every(av_made, b))
                if later(b):
                    eng.wait_ge(av_stored, at(av_stored, b, 0))
                for n in range(2):
                    eng.activation(weighed[:, n, :], att[n][:, :], ACT.Copy).then_inc(av_kept, 1)

            def copy_x2(b):
                eng.wait_ge(x2_made, every(x2_made, b))
                if later(b):
                    eng.wait_ge(fin_made, at(fin_made, b, 0))
                eng.activation(x2_kept[:, :, :], x2[:, :, :], ACT.Copy).then_inc(x2_copied, 1)

            def xn_back(b):
                eng.wait_ge(xn_tp, every(xn_tp, b))
                if later(b):
                    eng.wait_ge(hidden, at(hidden, b, 0))
                    eng.wait_ge(sim_made, at(sim_made, b, 0))
                eng.activation(xn_t[:, :], misc[0][:, 0:T], ACT.Copy).then_inc(xn_t_made, 1)

            def sim_back(b, j):
                eng.wait_ge(unit_step, every(unit_step, b))
                if later(b):
                    eng.wait_ge(select_step, at(select_step, b, 0))
                    eng.wait_ge(sim_low, at(sim_low, b, 0))
                eng.activation(sim[:, j, :], misc[1 - j][:, :], ACT.Copy,
                               scale=unit_inv[:, j:j + 1]).then_inc(sim_kept, 1)
                eng.wait_ge(sim_kept, at(sim_kept, b, j + 1))
                if later(b):
                    eng.wait_ge(piece_tp, at(piece_tp, b, 0))
                v = sim[:, j, :].rearrange("p (h k) -> p h k", h=FH)
                eng.activation(pieces[:, j, :, 0, :], v, ACT.Copy).then_inc(sim_high, 1)

            def pieces_back(b, j):
                eng.wait_ge(piece_tp, at(piece_tp, b, j + 1))
                if later(b):
                    eng.wait_ge(scores_made, at(scores_made, b, 0))
                eng.activation(pieces_t[:, j, :, :].rearrange("p h t -> p (h t)"),
                               misc[j][:, :].bitcast(FP16), ACT.Copy).then_inc(piece_t_made, 1)

            def activate(b, n):
                eng.wait_ge(hidden, at(hidden, b, n + 1))
                if later(b):
                    eng.wait_ge(gated, at(gated, b, 0))
                eng.activation(act_t[:, 4 * n:4 * n + 4, :].rearrange("p c t -> p (c t)"),
                               score[n][:, :], ACT.Gelu).then_inc(act_made, 1)

            def best_exp(b, j):
                eng.wait_ge(shifted_made, at(shifted_made, b, j + 1))
                eng.wait_ge(unit_made, every(unit_made, b))
                eng.activation(exps[:, j, :, :].rearrange("p h k -> p (h k)"),
                               shifted[:, j, :, :].rearrange("p h k -> p (h k)"), ACT.Exp,
                               scale=unit[:, j:j + 1]).then_inc(exps_made, 1)

            def log_sum(b):
                eng.wait_ge(total_made, every(total_made, b))
                eng.activation(log_total[:, :, :], total[:, :, :], ACT.Ln).then_inc(log_made, 1)

            def threshold(b):
                eng.wait_ge(cut_arg_made, every(cut_arg_made, b))
                eng.activation(cut_prob[:, :, :], cut_arg[:, :, :], ACT.Exp).then_inc(cut_prob_made, 1)

            def pair_probs(b, j, h):
                g = j * FH + h
                eng.wait_ge(scores_made, at(scores_made, b, g + 1))
                if later(b):
                    eng.wait_ge(acc_added, at(acc_added, b - 1, j * (FH - 1) + max(h, 1)))
                elif g == 0:
                    eng.wait_ge(setup_dve, 3)
                eng.activation(prob[:, g, :], score[g % 2][:, :], ACT.Exp, bias=neg_lse[:, j, h:h + 1],
                               scale=unit[:, j:j + 1]).then_inc(prob_made, 1)

            def prologue():
                xhat_back(0)
                qk_high_piece(0)
                v_back(0)
                copy_v(0)
                qk_middle_piece(0)
                max_back(0)
                for u in range(MAX_STEPS):
                    att_exp(0, u)
                weighed_back(0)
                xhat_back(1)
                qk_high_piece(1)
                v_back(1)
                qk_middle_piece(1)
                xn_back(0)
                sim_back(0, 0)
                sim_back(0, 1)

            def iteration(i, d, f, a, p):
                if a:
                    copy_v(i + 1)
                if f:
                    pieces_back(i, 0)
                    pieces_back(i, 1)
                if a:
                    max_back(i + 1)
                    for u in range(MAX_STEPS):
                        att_exp(i + 1, u)
                    weighed_back(i + 1)
                if f:
                    activate(i, 0)
                    activate(i, 1)
                    best_exp(i, 0)
                    best_exp(i, 1)
                    copy_x2(i)
                    log_sum(i)
                    threshold(i)
                if p:
                    xhat_back(i + 2)
                if f:
                    pair_probs(i, 0, 0)
                    pair_probs(i, 0, 1)
                if p:
                    qk_high_piece(i + 2)
                    v_back(i + 2)
                if f:
                    pair_probs(i, 0, 2)
                if p:
                    qk_middle_piece(i + 2)
                if f:
                    pair_probs(i, 0, 3)
                if a:
                    xn_back(i + 1)
                if f:
                    pair_probs(i, 0, 4)
                    pair_probs(i, 0, 5)
                if a:
                    sim_back(i + 1, 0)
                    sim_back(i + 1, 1)
                if f:
                    pair_probs(i, 0, 6)
                    pair_probs(i, 0, 7)
                    for h in range(FH):
                        pair_probs(i, 1, h)

            schedule(eng, prologue, iteration)

        @block.vector
        def _(eng):

            def ln1(b):
                eng.wait_ge(x_in, every(x_in, b))
                for j in range(TILES):
                    eng.bn_stats(stat1[:, j, :], xin[:, j, :]).then_inc(ln1_step, 1)
                value = held(eng, at(ln1_step, b, TILES))
                eng.wait_ge(setup_dve, 1)
                eng.wait_ge(ln1_step, value)
                for j in range(TILES):
                    eng.bn_aggr(mv1[:, j, :], stat1[:, j, :]).then_inc(ln1_step, 1)
                eng.wait_ge(ln1_step, at(ln1_step, b, 2 * TILES))
                if later(b):
                    eng.wait_ge(rstd1_made, at(rstd1_made, b, 0))
                eng.tensor_scalar(ln_tmp[:, :], mv1[:, :, 1], LN_EPS, None, ALU.add).then_inc(ln1_step, 1)

            def make_xhat(b):
                eng.wait_ge(rstd1_made, every(rstd1_made, b))
                eng.wait_ge(ln1_step, every(ln1_step, b))
                if later(b):
                    eng.wait_ge(xhat_tp, at(xhat_tp, b, 0))
                for j in range(TILES):
                    eng.tensor_scalar(xhat[:, j, :], xin[:, j, :], mv1[:, j, 0:1], rstd1[:, j:j + 1],
                                      ALU.subtract, ALU.mult).then_inc(xhat_made, 1)

            def qk_remainder(b):
                eng.wait_ge(qk_high, every(qk_high, b))
                eng.wait_ge(qk_made, every(qk_made, b))
                if later(b):
                    eng.wait_ge(qk_low, at(qk_low, b, 0))
                eng.tensor_tensor(qk_rest[:, :], misc[1][:, :], qk_piece[:, 0, :],
                                  ALU.subtract).then_inc(qk_rest_made, 1)

            def take_max(b, u):
                eng.wait_ge(max_scores, at(max_scores, b, u + 1))
                if u == 0:
                    if later(b):
                        eng.wait_ge(max_tp, at(max_tp, b, 0))
                if u < 4:
                    dst, src = neg_max[:, 4 * u:4 * u + 4, 0], att[u % 2][:, :].rearrange("p (h k) -> p h k", h=4)
                else:
                    dst = neg_max[:, 2 * (u - 4):2 * (u - 3), 1]
                    src = att[u % 2][:, :].rearrange("p (h k) -> p h k", h=2)
                eng.tensor_reduce(dst, src, AX.X, ALU.max, negate=True).then_inc(max_taken, 1)

            def make_y(b):
                if later(b):
                    eng.wait_ge(proj_made, at(proj_made, b, 0))
                eng.wait_ge(y_loaded, every(y_loaded, b))
                eng.reciprocal(recip[:, :], y_in[:, 1, :]).then_inc(recip_made, 1)
                eng.wait_ge(recip_made, every(recip_made, b))
                eng.tensor_tensor(y_t[:, :], y_in[:, 0, :], recip[:, :], ALU.mult).then_inc(y_t_made, 1)

            def make_x2(b):
                eng.wait_ge(proj_made, every(proj_made, b))
                eng.wait_ge(xres_in, every(xres_in, b))
                if later(b):
                    eng.wait_ge(x2_copied, at(x2_copied, b, 0))
                if later(b):
                    eng.wait_ge(xn_made, at(xn_made, b, 0))
                eng.tensor_tensor(x2[:, :, :].rearrange("p j d -> p (j d)"),
                                  xres[:, :, :].rearrange("p j d -> p (j d)"),
                                  att[1][:, 0:TILES * D], ALU.add).then_inc(x2_made, 1)
                eng.wait_ge(x2_made, every(x2_made, b))
                if later(b):
                    eng.wait_ge(scale2_made, at(scale2_made, b, 0))
                for j in range(TILES):
                    eng.bn_stats(stat2[:, j, :], x2[:, j, :]).then_inc(ln2_step, 1)
                value = held(eng, at(ln2_step, b, TILES))
                eng.wait_ge(setup_dve, 1)
                eng.wait_ge(ln2_step, value)
                for j in range(TILES):
                    eng.bn_aggr(mv2[:, j, :], stat2[:, j, :]).then_inc(ln2_step, 1)
                eng.wait_ge(ln2_step, at(ln2_step, b, 2 * TILES))
                eng.tensor_scalar(bounded[:, :], mv2[:, :, 1], LN_EPS, 1e-24 / D, ALU.add,
                                  ALU.mult).then_inc(ln2_step, 1)
                eng.wait_ge(ln2_step, at(ln2_step, b, 2 * TILES + 1))
                eng.tensor_tensor(bounded[:, :], mv2[:, :, 1], bounded[:, :], ALU.max).then_inc(ln2_step, 1)

            def make_xn(b):
                eng.wait_ge(scale2_made, every(scale2_made, b))
                eng.wait_ge(ln2_step, every(ln2_step, b))
                if later(b):
                    eng.wait_ge(xn_tp, at(xn_tp, b, 0))
                for j in range(TILES):
                    eng.tensor_scalar(xn[:, j, :], x2[:, j, :], mv2[:, j, 0:1], scale2[:, j:j + 1],
                                      ALU.subtract, ALU.mult).then_inc(xn_made, 1)

            def select(b, j):
                n = j * SELECT
                value = held(eng, at(sim_kept, b, j + 1))
                eng.wait_ge(setup_dve, 1)
                eng.wait_ge(sim_kept, value)
                keys_of = [sim[:, j, l * KEYS:(l + 1) * KEYS] for l in range(LISTS)]
                for l in range(LISTS):
                    eng.max(top[:, l, 0:8], keys_of[l]).then_inc(select_step, 1)
                    n += 1
                value = held(eng, at(select_step, b, n))
                eng.wait_ge(setup_dve, 1)
                eng.wait_ge(select_step, value)
                for l in range(LISTS):
                    eng.match_replace(left[:, l, :], top[:, l, 0:8], keys_of[l], LOWEST).then_inc(select_step, 1)
                    n += 1
                value = held(eng, at(select_step, b, n))
                eng.wait_ge(setup_dve, 1)
                eng.wait_ge(select_step, value)
                for l in range(LISTS):
                    eng.max(top[:, l, 8:16], left[:, l, :]).then_inc(select_step, 1)
                    n += 1
                value = held(eng, at(select_step, b, n))
                eng.wait_ge(setup_dve, 1)
                eng.wait_ge(select_step, value)
                col = 0
                for a0, na, nb in PAIR_BLOCKS:
                    dst = cand[:, :, col:col + na * nb].rearrange("p h (a b) -> p h a b", b=nb)
                    xs = top[:, 0:LISTS:2, a0:a0 + na].unsqueeze(3).broadcast_to([P, FH, na, nb])
                    ys = top[:, 1:LISTS:2, 0:nb].unsqueeze(2).broadcast_to([P, FH, na, nb])
                    eng.tensor_tensor(dst, xs, ys, ALU.add).then_inc(select_step, 1)
                    n += 1
                    col += na * nb
                ends = top[:, :, 0:TOPK:TOPK - 1].rearrange("p (h a) e -> p h a e", a=2)
                eng.tensor_reduce(size[:, j, :], ends, AX.XY, ALU.add, apply_absolute_value=True).then_inc(select_step, 1)
                n += 1
                value = held(eng, at(select_step, b, n))
                eng.wait_ge(setup_dve, 1)
                eng.wait_ge(select_step, value)
                for h in range(FH):
                    eng.max(best[:, j, h, 0:8], cand[:, h, :]).then_inc(select_step, 1)
                    n += 1
                value = held(eng, at(select_step, b, n))
                eng.wait_ge(setup_dve, 1)
                eng.wait_ge(select_step, value)
                for h in range(FH):
                    eng.match_replace(cand_left[:, h, :], best[:, j, h, 0:8], cand[:, h, :], LOWEST).then_inc(select_step, 1)
                    n += 1
                value = held(eng, at(select_step, b, n))
                eng.wait_ge(setup_dve, 1)
                eng.wait_ge(select_step, value)
                for h in range(FH):
                    eng.max(best[:, j, h, 8:16], cand_left[:, h, :]).then_inc(select_step, 1)
                    n += 1
                value = held(eng, at(select_step, b, n))
                eng.wait_ge(setup_dve, 1)
                eng.wait_ge(select_step, value)
                eng.scalar_tensor_tensor(cut[:, j, :], size[:, j, :], -float(2 ** -21), best[:, j, :, TOPK - 1],
                                         ALU.mult, ALU.add).then_inc(select_step, 1)
                n += 1
                eng.tensor_tensor(shifted[:, j, :, :], best[:, j, :, :],
                                  best[:, j, :, 0:1].broadcast_to([P, FH, TOPK]),
                                  ALU.subtract).then_inc(shifted_made, 1)

            def sum_best(b):
                eng.wait_ge(exps_made, every(exps_made, b))
                eng.tensor_reduce(total[:, :, :], exps[:, :, :, :], AX.X, ALU.add).then_inc(total_made, 1)

            def log_sum_exp(b):
                if later(b):
                    eng.wait_ge(prob_made, at(prob_made, b, 0))
                eng.wait_ge(log_made, every(log_made, b))
                for j in range(TILES):
                    eng.scalar_tensor_tensor(neg_lse[:, j, :], best[:, j, :, 0], neg_unit[:, j:j + 1],
                                             log_total[:, j, :], ALU.mult, ALU.subtract).then_inc(lse_step, 1)
                eng.wait_ge(select_step, every(select_step, b))
                eng.wait_ge(lse_step, every(lse_step, b))
                for j in range(TILES):
                    eng.scalar_tensor_tensor(cut_arg[:, j, :], cut[:, j, :], unit[:, j:j + 1],
                                             neg_lse[:, j, :], ALU.mult, ALU.add).then_inc(cut_arg_made, 1)

            def make_unit_next(b):
                for j in range(TILES):
                    eng.wait_ge(sim_made, at(sim_made, b, j + 1))
                    if j == 0 and later(b):
                        eng.wait_ge(sim_kept, at(sim_kept, b, 0))
                        eng.wait_ge(unit_made, at(unit_made, b, 0))
                    eng.tensor_reduce(peak[:, j:j + 1], misc[1 - j][:, :], AX.X, ALU.max,
                                      apply_absolute_value=True).then_inc(unit_step, 1)
                eng.wait_ge(unit_step, at(unit_step, b, TILES))
                eng.tensor_scalar(unit_next[:, :], peak[:, :], 1e-30, 1 / SIM_PEAK, ALU.max,
                                  ALU.mult).then_inc(unit_step, 1)
                eng.wait_ge(unit_step, at(unit_step, b, TILES + 1))
                eng.reciprocal(unit_inv[:, :], unit_next[:, :]).then_inc(unit_step, 1)

            def make_unit(b):
                eng.wait_ge(unit_step, every(unit_step, b))
                if later(b):
                    eng.wait_ge(prob_made, at(prob_made, b, 0))
                    eng.wait_ge(cut_arg_made, at(cut_arg_made, b, 0))
                eng.tensor_scalar(unit[:, :], unit_next[:, :], 1.0, None, ALU.mult).then_inc(unit_made, 1)
                eng.tensor_scalar(neg_unit[:, :], unit_next[:, :], -1.0, None, ALU.mult).then_inc(unit_made, 1)

            def mask(b, j, h):
                g = j * FH + h
                if g == 0:
                    eng.wait_ge(cut_prob_made, every(cut_prob_made, b))
                eng.wait_ge(prob_made, at(prob_made, b, g + 1))
                eng.scalar_tensor_tensor(prob[:, g, :], prob[:, g, :], cut_prob[:, j, h:h + 1], prob[:, g, :],
                                         ALU.is_ge, ALU.mult).then_inc(prob_masked, 1)

            def gate(b):
                eng.wait_ge(act_made, every(act_made, b))
                if later(b):
                    eng.wait_ge(down_made, at(down_made, b, 0))
                for j in range(TILES):
                    eng.wait_ge(acc_tp, at(acc_tp, b, j + 1))
                    toks = slice(j * P, (j + 1) * P)
                    eng.tensor_tensor(gated_t[:, :, toks], score[j][:, :].rearrange("p (c t) -> p c t", t=P),
                                      act_t[:, :, toks], ALU.mult).then_inc(gated, 1)

            def finish(b):
                eng.wait_ge(down_made, every(down_made, b))
                eng.wait_ge(x2_copied, every(x2_copied, b))
                if later(b):
                    eng.wait_ge(out_stored, at(out_stored, b, 0))
                eng.tensor_tensor(fin[:, :, :].rearrange("p j d -> p (j d)"),
                                  x2_kept[:, :, :].rearrange("p j d -> p (j d)"),
                                  att[0][:, 0:TILES * D], ALU.add).then_inc(fin_made, 1)

            def prologue():
                eng.wait_ge(consts_in, 32)
                eng.tensor_copy(cb[:, :], consts_f[:, 0:SEL]).then_inc(setup_dve, 1)
                eng.tensor_copy(ident_h[:, :], consts_f[:, 0:P]).then_inc(setup_dve, 1)
                eng.tensor_copy(sel[:, :], consts_f[:, SEL:SEL + EXPERTS]).then_inc(setup_dve, 1)
                ln1(0)
                make_xhat(0)
                eng.wait_ge(weights_in, 7 * 16)
                eng.tensor_scalar(wdt[:, :], wdt[:, :], gam[:, 0:1], None, ALU.mult).then_inc(setup_done, 1)
                eng.wait_ge(wkey_made, 1)
                eng.tensor_scalar(wkey[:, :], misc[1][:, :], gam[:, 0:1], None, ALU.mult).then_inc(setup_done, 1)
                qk_remainder(0)
                for u in range(MAX_STEPS):
                    take_max(0, u)
                ln1(1)
                make_xhat(1)
                qk_remainder(1)
                make_y(0)
                make_x2(0)
                make_xn(0)
                make_unit_next(0)

            def iteration(i, d, f, a, p):
                if a:
                    for u in range(MAX_STEPS):
                        take_max(i + 1, u)
                if f:
                    make_unit(i)
                    select(i, 0)
                if d:
                    gate(i - 1)
                if f:
                    select(i, 1)
                if a:
                    make_y(i + 1)
                if d:
                    finish(i - 1)
                if p:
                    ln1(i + 2)
                if f:
                    sum_best(i)
                if a:
                    make_x2(i + 1)
                if f:
                    log_sum_exp(i)
                if p:
                    make_xhat(i + 2)
                if f:
                    mask(i, 0, 0)
                    mask(i, 0, 1)
                if p:
                    qk_remainder(i + 2)
                if f:
                    mask(i, 0, 2)
                if a:
                    make_xn(i + 1)
                if f:
                    mask(i, 0, 3)
                    mask(i, 0, 4)
                if a:
                    make_unit_next(i + 1)
                if f:
                    for h in range(5, FH):
                        mask(i, 0, h)
                    for h in range(FH):
                        mask(i, 1, h)

            schedule(eng, prologue, iteration)

        @block.tensor
        def _(eng):
            def fold_keys():
                eng.wait_ge(weights_in, 7 * 16)
                for l in range(LISTS):
                    ins = eng.matmul(misc[1][:, l * KEYS:(l + 1) * KEYS], wqs[:, l, :],
                                     keyt[:, l * KEYS:(l + 1) * KEYS], start=True, stop=True)
                ins.then_inc(wkey_made, 1)

            def two_transposes(bank, src, sig):
                for j in range(TILES):
                    ins = eng.transpose(bank[:, j * P:(j + 1) * P], src[:, j, :], ident[:, :])
                ins.then_inc(sig, 1)

            def xhat_transpose(b, reader, of_batch):
                eng.wait_ge(xhat_made, every(xhat_made, b))
                eng.wait_ge(reader, every(reader, of_batch))
                two_transposes(misc[0], xhat, xhat_tp)

            def project_qkv(b, reader, of_batch):
                eng.wait_ge(xhat_t_made, every(xhat_t_made, b))
                eng.wait_ge(reader, every(reader, of_batch))
                eng.matmul(misc[1][:, 0:T], wa[:, 0:D], xhat_t[:, :], start=True, stop=True)
                eng.matmul(misc[1][:, T:2 * T], wa[:, 2 * HD:D + 2 * HD], xhat_t[:, :],
                           start=True, stop=True).then_inc(qk_made, 1)
                for j in range(TILES):
                    ins = eng.matmul(misc[0][:, j * HD:(j + 1) * HD], xhat_t[:, j * P:(j + 1) * P],
                                     wa[:, D + HD:D + 2 * HD], start=True, stop=True)
                ins.then_inc(v_made, 1)

            def scores_for_max(b, u):
                if u == 0:
                    if later(b):
                        eng.wait_ge(av_kept, at(av_kept, b, 0))
                    if not isinstance(b, int) or b >= 2:
                        eng.wait_ge(prob_masked, at(prob_masked, b - 2, 1))
                    eng.wait_ge(stack_in, every(stack_in, b))
                elif u == 1:
                    if later(b):
                        eng.wait_ge(x2_made, at(x2_made, b, 0))
                else:
                    eng.wait_ge(max_taken, at(max_taken, b, u - 1))
                bank = att[u % 2]
                nh, nk, h0, j = (4, P, 4 * u, 0) if u < 4 else (2, T, 2 * (u - 4), 1)
                eng.matmul(bank[:, :], ident_bf, mask_q0 if j == 0 else mask_q1, start=True, stop=False)
                for n in range(nh):
                    ins = eng.matmul(bank[:, n * nk:(n + 1) * nk], q_stack[0:STACK, h0 + n, j * P:(j + 1) * P],
                                     k_stack[0:STACK, 0:nk], start=False, stop=n == nh - 1)
                ins.then_inc(max_scores, 1)

            def max_transpose(b):
                eng.wait_ge(max_taken, every(max_taken, b))
                if later(b):
                    eng.wait_ge(piece_t_made, at(piece_t_made, b - 1, 1))
                else:
                    eng.wait_ge(v_next_made, every(v_next_made, b))
                eng.transpose(misc[0][0:H * TILES, 0:P], neg_max[:, :, :].rearrange("p h j -> p (h j)"),
                              ident[:, :]).then_inc(max_tp, 1)

            def scores_for_probs(b, u):
                if u == 0:
                    eng.wait_ge(max_row_in, every(max_row_in, b))
                    if not later(b):
                        eng.wait_ge(ones_in, 16)
                if u < 2:
                    eng.wait_ge(max_taken, every(max_taken, b))
                else:
                    eng.wait_ge(att_probs, at(att_probs, b, u - 1))
                bank = att[u % 2]
                if u < 8:
                    m, k, q = mask_t0, k_stack[:, 0:P], q_stack[:, 2 * u:2 * u + 2, :]
                else:
                    m, k, q = mask_t1, k_stack[:, P:T], q_stack[:, 4 * (u - 8):4 * (u - 7), P:T]
                eng.matmul(bank[:, :], ident_bf, m, start=True, stop=False)
                eng.matmul(bank[:, :], k, q, start=False, stop=True).then_inc(att_scores, 1)

            def weigh_values(b):
                eng.wait_ge(v_copied, every(v_copied, b))
                eng.wait_ge(att_probs, every(att_probs, b))
                for n in range(2):
                    for g in range(4):
                        h = 4 * g + 2 * n
                        eng.matmul(att[n][32 * g:32 * g + 32, :], v_cols[:, 0, :], probs0[:, h:h + 2, :],
                                   start=True, stop=False)
                    for g in range(4):
                        h = 4 * g + 2 * n
                        late = att[n][32 * g:32 * g + 32, :].rearrange("p (h t) -> p h t", t=T)[:, :, P:T]
                        ins = eng.matmul(late, v_cols[:, 1, :], probs1[:, h:h + 2, :], start=False, stop=True)
                ins.then_inc(av_made, 1)

            def project_y(b):
                eng.wait_ge(y_t_made, every(y_t_made, b))
                for j in range(TILES):
                    ins = eng.matmul(att[1][:, j * D:(j + 1) * D], y_t[:, j * P:(j + 1) * P], wp[:, :],
                                     start=True, stop=True)
                ins.then_inc(proj_made, 1)

            def xn_transpose(b, reader, of_batch):
                eng.wait_ge(xn_made, every(xn_made, b))
                eng.wait_ge(reader, every(reader, of_batch))
                two_transposes(misc[0], xn, xn_tp)

            def key_scores(b, reader, of_batch):
                eng.wait_ge(reader, every(reader, of_batch))
                eng.wait_ge(xn_t_made, every(xn_t_made, b))
                for j in range(TILES):
                    eng.matmul(misc[1 - j][:, :], xn_t[:, j * P:(j + 1) * P], wkey[:, :],
                               start=True, stop=True).then_inc(sim_made, 1)

            def hidden_chunks(b, n):
                if later(b):
                    eng.wait_ge(gated, at(gated, b - 1, n + 1))
                for c in range(4 * n, 4 * n + 4):
                    ins = eng.matmul(score[n][:, (c % 4) * T:(c % 4 + 1) * T], wdt[:, c * P:(c + 1) * P],
                                     xn_t[:, :], start=True, stop=True)
                ins.then_inc(hidden, 1)

            def piece_transposes(b, j):
                eng.wait_ge(sim_kept, every(sim_kept, b))
                eng.wait_ge(sim_low, at(sim_low, b, j + 1))
                dst = misc[j][:, :].bitcast(FP16)
                for h in range(FH):
                    ins = eng.transpose(dst[:, h * P:(h + 1) * P],
                                        pieces[:, j, h, :, :].rearrange("p s k -> p (s k)"), ident_h[:, :])
                ins.then_inc(piece_tp, 1)

            def pair_scores(b, j, h):
                g = j * FH + h
                if h == 0:
                    eng.wait_ge(piece_t_made, at(piece_t_made, b, j + 1))
                if g < 2:
                    eng.wait_ge(act_made, at(act_made, b, g + 1))
                else:
                    eng.wait_ge(prob_made, at(prob_made, b, g - 1))
                for half in range(2):
                    cols = slice(half * BANK, (half + 1) * BANK)
                    ins = eng.matmul(score[g % 2][:, cols], pieces_t[:, j, h, :], sel[:, cols],
                                     start=True, stop=True)
                ins.then_inc(scores_made, 1)

            def acc_transposes(b, j):
                eng.wait_ge(prob_made, at(prob_made, b, TILES * FH - 1 + j))
                eng.wait_ge(acc_added, at(acc_added, b, (FH - 1) * (j + 1)))
                for c in range(CH):
                    ins = eng.transpose(score[j][:, c * P:(c + 1) * P], acc[:, j, c * P:(c + 1) * P], ident[:, :])
                ins.then_inc(acc_tp, 1)

            def expert_output(b, a):
                if a:
                    eng.wait_ge(av_kept, at(av_kept, b + 2, 1))
                else:
                    eng.wait_ge(fin_made, every(fin_made, b - 1))
                eng.wait_ge(gated, every(gated, b))
                for j in range(TILES):
                    for c in range(CH):
                        ins = eng.matmul(att[0][:, j * D:(j + 1) * D], gated_t[:, c, j * P:(j + 1) * P],
                                         wu[:, c, :], start=c == 0, stop=c == CH - 1)
                ins.then_inc(down_made, 1)

            def prologue():
                eng.wait_ge(consts_in, 32)
                xhat_transpose(0, setup_pool, 0)
                fold_keys()
                project_qkv(0, setup_done, 0)
                eng.wait_ge(setup_dve, 3)
                for u in range(MAX_STEPS):
                    scores_for_max(0, u)
                max_transpose(0)
                for u in range(MAX_STEPS):
                    scores_for_probs(0, u)
                weigh_values(0)
                xhat_transpose(1, max_t_made, 0)
                project_qkv(1, qk_rest_made, 0)
                project_y(0)
                xn_transpose(0, v_next_made, 1)
                key_scores(0, qk_rest_made, 1)

            def iteration(i, d, f, a, p):
                if a:
                    scores_for_max(i + 1, 0)
                    scores_for_max(i + 1, 1)
                if f:
                    piece_transposes(i, 0)
                if a:
                    scores_for_max(i + 1, 2)
                    scores_for_max(i + 1, 3)
                if f:
                    piece_transposes(i, 1)
                if a:
                    for u in range(4, MAX_STEPS):
                        scores_for_max(i + 1, u)
                    max_transpose(i + 1)
                if d:
                    acc_transposes(i - 1, 0)
                if a:
                    for u in range(MAX_STEPS):
                        scores_for_probs(i + 1, u)
                if d:
                    acc_transposes(i - 1, 1)
                if a:
                    weigh_values(i + 1)
                if f:
                    hidden_chunks(i, 0)
                    hidden_chunks(i, 1)
                if d:
                    expert_output(i - 1, a)
                if f:
                    pair_scores(i, 0, 0)
                    pair_scores(i, 0, 1)
                if a:
                    project_y(i + 1)
                if p:
                    xhat_transpose(i + 2, max_t_made, i + 1)
                    project_qkv(i + 2, piece_t_made, i)
                if f:
                    pair_scores(i, 0, 2)
                    pair_scores(i, 0, 3)
                if a:
                    if p:
                        xn_transpose(i + 1, v_next_made, i + 2)
                    else:
                        xn_transpose(i + 1, max_t_made, i + 1)
                if f:
                    pair_scores(i, 0, 4)
                    pair_scores(i, 0, 5)
                if a:
                    if p:
                        key_scores(i + 1, qk_rest_made, i + 2)
                    else:
                        key_scores(i + 1, piece_t_made, i)
                if f:
                    pair_scores(i, 0, 6)
                    pair_scores(i, 0, 7)
                    for h in range(FH):
                        pair_scores(i, 1, h)

            schedule(eng, prologue, iteration)


def constants():
    import numpy as np
    eye = np.eye(P, dtype=np.float32)
    q, k = np.arange(P)[:, None], np.arange(P)[None, :]
    tri = np.where(k > q, np.float32(MASKED), np.float32(0))
    none = np.zeros((P, P), np.float32)
    masks = [np.tile(tri, (1, 4)), np.tile(np.hstack([none, tri]), (1, 2)),
             np.tile(np.hstack([tri.T, none]), (1, 2)), np.tile(tri.T, (1, 4))]
    pair = np.arange(EXPERTS)
    spread = np.concatenate([(np.arange(KEYS)[:, None] == pair // KEYS),
                             (np.arange(KEYS)[:, None] == pair % KEYS)]).astype(np.float32)
    return np.hstack([eye] + masks + [np.ones((P, T), np.float32), np.vstack([spread, spread])])


def kernel(L0_attn_x, L0_attn_w_attn, L0_attn_w_proj, L0_ffn_gamma, L0_ffn_wq, L0_ffn_keys,
           L0_ffn_table_down, L0_ffn_table_up):
    import numpy as np
    import concourse.bacc as bacc
    from concourse.bass_utils import run_bass_kernel_spmd

    arrays = {
        "x": np.asarray(L0_attn_x),
        "w_attn": np.asarray(L0_attn_w_attn),
        "w_proj": np.asarray(L0_attn_w_proj),
        "gamma": np.asarray(L0_ffn_gamma).reshape(D, 1),
        "wq": np.asarray(L0_ffn_wq).reshape(2, FH, DK, D).transpose(2, 1, 0, 3).reshape(DK, LISTS, D),
        "keys": np.asarray(L0_ffn_keys).transpose(3, 0, 2, 1).reshape(DK, LISTS * KEYS),
        "down": np.asarray(L0_ffn_table_down)[:EXPERTS].T,
        "up": np.asarray(L0_ffn_table_up)[:EXPERTS],
        "consts": constants(),
    }
    arrays = {n: np.ascontiguousarray(a) for n, a in arrays.items()}
    nc = bacc.Bacc("TRN2", target_bir_lowering=False, num_devices=1)
    args = [nc.dram_tensor(n, a.shape, mybir.dt.from_np(a.dtype), kind="ExternalInput").ap()
            for n, a in arrays.items()]
    out = nc.dram_tensor("out", (BATCHES, T, D), FP32, kind="ExternalOutput").ap()
    build(nc, *args, out)
    result = run_bass_kernel_spmd(nc, [arrays], core_ids=[0])
    return result.results[0]["out"]
```

```python
import concourse.bass as bass
from concourse import mybir
from contextlib import ExitStack

FP32 = mybir.dt.float32
BF16 = mybir.dt.bfloat16
FP16 = mybir.dt.float16
ALU = mybir.AluOpType
ACT = mybir.ActivationFunctionType
AX = mybir.AxisListType

P = 128
BATCHES, T, D = 16, 256, 128
TILES = T // P
H, HD = 16, 8
FH, KEYS, DK = 8, 32, 64
EXPERTS = KEYS * KEYS
CH = EXPERTS // P
TOPK = 16
LISTS = 2 * FH
LN_EPS = 1e-5
MASKED = -float(2 ** 100)
LOWEST = -3.0e38
SIM_PEAK = float(2 ** 15)
Q_PIECE = (0, 0, 0, 1, 1, 2)
K_PIECE = (0, 1, 2, 0, 1, 0)
STACK = len(Q_PIECE) * HD
PAIR_BLOCKS = ((0, 1, 16), (1, 1, 8), (2, 2, 5), (4, 4, 3), (8, 8, 1))
PAIRS = sum(na * nb for _, na, nb in PAIR_BLOCKS)
BANK = 512
MAX_STEPS = 12


def later(batch):
    return not isinstance(batch, int) or batch > 0


def held(eng, value):
    return value if isinstance(value, int) else eng.to_reg(value)


def build(nc, x, w_attn, w_proj, gamma, wq, keys, down, up, consts, out):
    ctx = ExitStack()
    with ctx:
        def sb(name, shape, dt=FP32):
            return ctx.enter_context(nc.sbuf_tensor(name, shape, dt))

        raised = {}

        def signal(name, per_batch=1):
            sem = ctx.enter_context(nc.semaphore(name))
            raised[sem] = per_batch
            return sem

        def at(sem, batch, n):
            return batch * raised[sem] + n

        def every(sem, batch):
            return at(sem, batch, raised[sem])

        q_scratch = nc.dram_tensor("q_scratch", (P, 3, T), BF16, kind="Internal").ap()

        SEL = P + 2 * BANK + T
        ident = sb("ident", [P, P])
        cb = sb("cb", [P, SEL], BF16)
        ident_bf = cb[:, 0:P]
        mask_q = cb[:, P:P + BANK].rearrange("p (n k) -> p n k", k=P)
        mask_t = cb[:, P + BANK:P + 2 * BANK].rearrange("p (n k) -> p n k", k=P)
        ones_row = cb[0:1, P + 2 * BANK:SEL]
        ident_h = sb("ident_h", [P, P], FP16)
        sel = sb("sel", [P, EXPERTS], FP16)
        wa = sb("wa", [P, D + 2 * HD])
        wp = sb("wp", [P, D])
        gam = sb("gam", [P, 1])
        wkey = sb("wkey", [P, LISTS * KEYS])
        wdt = sb("wdt", [P, EXPERTS])
        wu = sb("wu", [P, CH, D])

        xin = sb("xin", [P, TILES, D])
        stat1 = sb("stat1", [P, TILES, 6])
        mv1 = sb("mv1", [P, TILES, 2])
        rstd1 = sb("rstd1", [P, TILES])
        half_neg = sb("half_neg", [P, TILES])
        ln_tmp = sb("ln_tmp", [P, TILES])
        xhat = sb("xhat", [P, TILES, D])
        xhat_t = sb("xhat_t", [P, T])
        qk_piece = sb("qk_piece", [P, 3, 2 * T], BF16)
        qk_rest = sb("qk_rest", [P, 2 * T])
        v_next = sb("v_next", [P, TILES, HD])
        q_stack = sb("q_stack", [STACK + 1, H, T], BF16)
        k_stack = sb("k_stack", [STACK + 1, T], BF16)
        v_blocks = sb("v_blocks", [P, TILES, 4 * (32 + HD)])
        one_blocks = sb("one_blocks", [P, 4 * (32 + HD)])
        late_scores = sb("late_scores", [P, H, T], BF16)
        halves = [sb("halves", [P, H, TILES, P], BF16)]
        row = late_scores[:, :, :].rearrange("p h t -> p (h t)")
        for w in (64, 32, 16, 8):
            halves.append(row[:, 0:H * TILES * w].rearrange("p (h j k) -> p h j k", h=H, j=TILES))
            row = row[:, H * TILES * w:]
        neg_max = sb("neg_max", [P, H, TILES])
        max_t = sb("max_t", [H * TILES, P], BF16)
        probs0 = sb("probs0", [P, H, T])
        probs1 = sb("probs1", [P, H, P])
        y_t = sb("y_t", [P, T])
        xres = sb("xres", [P, TILES, D])
        x2 = sb("x2", [P, TILES, D])
        x2_kept = sb("x2_kept", [P, TILES, D])
        stat2 = sb("stat2", [P, TILES, 6])
        mv2 = sb("mv2", [P, TILES, 2])
        bounded = sb("bounded", [P, TILES])
        scale2 = sb("scale2", [P, TILES])
        xn = sb("xn", [P, TILES, D])
        xn_t = sb("xn_t", [P, T])
        sim = sb("sim", [P, TILES, LISTS * KEYS])
        unit = sb("unit", [P, 1])
        neg_unit = sb("neg_unit", [P, 1])
        unit_inv = sb("unit_inv", [P, 1])
        pieces = sb("pieces", [P, TILES, FH, 2, 2 * KEYS], FP16)
        pieces_t = sb("pieces_t", [P, TILES, FH, P], FP16)
        top = sb("top", [P, LISTS, TOPK])
        left = sb("left", [P, LISTS, KEYS])
        cand = sb("cand", [P, FH, PAIRS])
        cand_left = sb("cand_left", [P, FH, PAIRS])
        best = sb("best", [P, TILES, FH, TOPK])
        size = sb("size", [P, TILES, FH])
        cut = sb("cut", [P, TILES, FH])
        shifted = sb("shifted", [P, TILES, FH, TOPK])
        exps = sb("exps", [P, TILES, FH, TOPK])
        total = sb("total", [P, TILES, FH])
        log_total = sb("log_total", [P, TILES, FH])
        neg_lse = sb("neg_lse", [P, TILES, FH])
        cut_arg = sb("cut_arg", [P, TILES, FH])
        cut_prob = sb("cut_prob", [P, TILES, FH])
        prob = sb("prob", [P, TILES * FH, EXPERTS])
        acc = sb("acc", [P, TILES, EXPERTS])
        act_t = sb("act_t", [P, CH, T])
        gated_t = sb("gated_t", [P, CH, T])
        fin = sb("fin", [P, TILES, D])
        consts_f, wqs, keyt, wkey_sq, all_ones = [
            prob[:, :, :].rearrange("p a b -> p (a b)")[0:rows, end - width:end] for rows, width, end in (
                (P, SEL + EXPERTS, SEL + EXPERTS), (DK, LISTS * D, 6 * EXPERTS), (DK, LISTS * KEYS, 13 * BANK),
                (P, LISTS * KEYS, 14 * BANK), (P, P, 15 * BANK))]

        score = [ctx.enter_context(nc.psum_tensor(f"score{n}", [P, EXPERTS], FP32)) for n in range(2)]
        att = [ctx.enter_context(nc.psum_tensor(f"att{n}", [P, BANK], FP32)) for n in range(2)]
        misc = [ctx.enter_context(nc.psum_tensor(f"misc{n}", [P, BANK], FP32)) for n in range(2)]

        weights_in = signal("weights_in")
        wa_in = signal("wa_in")
        ident_in = signal("ident_in")
        consts_in = signal("consts_in")
        ones_in = signal("ones_in")
        setup_pool = signal("setup_pool", 5)
        setup_dve = signal("setup_dve")
        wkey_made = signal("wkey_made")
        wkey_read = signal("wkey_read")
        setup_done = signal("setup_done", 2)
        x_in = signal("x_in", 16)
        ln1_step = signal("ln1_step", 5)
        rstd1_made = signal("rstd1_made")
        x_centred = signal("x_centred")
        xhat_made = signal("xhat_made")
        xhat_tp = signal("xhat_tp")
        xhat_t_made = signal("xhat_t_made")
        qk_made = signal("qk_made")
        v_made = signal("v_made")
        qk_high = signal("qk_high")
        qk_rest_made = signal("qk_rest_made")
        qk_middle = signal("qk_middle")
        qk_low = signal("qk_low")
        v_next_made = signal("v_next_made")
        scratch_in = signal("scratch_in", 16)
        stack_in = signal("stack_in", 16 * 2 * len(Q_PIECE))
        max_scores = signal("max_scores", MAX_STEPS)
        max_kept = signal("max_kept", MAX_STEPS)
        max_step = signal("max_step", 6)
        max_tp = signal("max_tp")
        max_t_made = signal("max_t_made")
        max_row_in = signal("max_row_in", 16)
        att_scores = signal("att_scores", MAX_STEPS)
        att_probs = signal("att_probs", MAX_STEPS)
        v_copied = signal("v_copied")
        av_made = signal("av_made")
        y_inverse = signal("y_inverse")
        y_t_made = signal("y_t_made")
        proj_made = signal("proj_made")
        xres_in = signal("xres_in", 16)
        x2_made = signal("x2_made")
        ln2_step = signal("ln2_step", 6)
        scale2_made = signal("scale2_made")
        xn_made = signal("xn_made", 2)
        xn_tp = signal("xn_tp")
        xn_t_made = signal("xn_t_made")
        sim_made = signal("sim_made", 2)
        sim_kept = signal("sim_kept", 2)
        unit_step = signal("unit_step", 6)
        norms_made = signal("norms_made")
        sim_high = signal("sim_high", 2)
        sim_low = signal("sim_low", 2)
        piece_tp = signal("piece_tp", 2)
        piece_t_made = signal("piece_t_made", 2)
        hidden = signal("hidden", 2)
        act_made = signal("act_made", 2)
        SELECT = 3 * LISTS + len(PAIR_BLOCKS) + 1 + 3 * FH + 1
        select_step = signal("select_step", TILES * SELECT)
        shifted_made = signal("shifted_made", 2)
        exps_made = signal("exps_made", 2)
        total_made = signal("total_made", 2)
        log_made = signal("log_made", 2)
        lse_step = signal("lse_step", 2)
        cut_arg_made = signal("cut_arg_made", 2)
        cut_prob_made = signal("cut_prob_made", 2)
        scores_made = signal("scores_made", TILES * FH)
        prob_made = signal("prob_made", TILES * FH)
        prob_masked = signal("prob_masked", TILES * FH)
        acc_added = signal("acc_added", TILES * (FH - 1))
        late_added = signal("late_added", FH - 1)
        x2_copied = signal("x2_copied")
        acc_tp = signal("acc_tp", 2)
        gated = signal("gated", 2)
        down_made = signal("down_made", 2)
        fin_made = signal("fin_made")
        out_stored = signal("out_stored", 16)

        block = ctx.enter_context(nc.Block())

        def schedule(eng, prologue, iteration):
            prologue()
            iteration(0, d=False, f=True, a=True, p=True)
            with eng.Fori(1, BATCHES - 2) as i:
                iteration(i, d=True, f=True, a=True, p=True)
            iteration(BATCHES - 2, d=True, f=True, a=True, p=False)
            iteration(BATCHES - 1, d=True, f=True, a=False, p=False)
            iteration(BATCHES, d=True, f=False, a=False, p=False)

        @block.sync
        def _(eng):
            x_v = x.rearrange("b (j p) d -> b p j d", p=P)
            out_v = out.rearrange("b (j p) d -> b p j d", p=P)

            def load_x(b):
                value = held(eng, at(xhat_made, b, 0))
                if later(b):
                    eng.wait_ge(setup_dve, 1)
                    eng.wait_ge(xhat_made, value)
                eng.dma_start(xin[:, :, :], x_v[b]).then_inc(x_in, 16)

            def load_residual(b):
                value = held(eng, at(x2_made, b, 0))
                if later(b):
                    eng.wait_ge(setup_dve, 1)
                    eng.wait_ge(x2_made, value)
                eng.dma_start(xres[:, :, :], x_v[b]).then_inc(xres_in, 16)

            def stack_pieces(b):
                value = held(eng, every(qk_high, b))
                read = held(eng, at(stack_in, b, 0))
                used = held(eng, at(att_scores, b, 0))
                stored = held(eng, every(scratch_in, b))
                eng.wait_ge(qk_high, value)
                eng.wait_ge(qk_middle, value)
                eng.wait_ge(qk_low, value)
                if later(b):
                    eng.wait_ge(stack_in, read)
                eng.dma_start(q_scratch, qk_piece[:, :, 0:T]).then_inc(scratch_in, 16)
                if later(b):
                    eng.wait_ge(att_scores, used)
                for c in range(len(K_PIECE)):
                    eng.dma_start(k_stack[c * HD:(c + 1) * HD, :],
                                  qk_piece[D - 2 * HD:D - HD, K_PIECE[c], T:2 * T]).then_inc(stack_in, 16)
                eng.wait_ge(scratch_in, stored)
                view = q_scratch.rearrange("(h d) s t -> s d h t", d=HD)
                for c in range(len(Q_PIECE)):
                    eng.dma_start(q_stack[c * HD:(c + 1) * HD, :, :], view[Q_PIECE[c]]).then_inc(stack_in, 16)

            def place_max_row(b):
                value = held(eng, every(max_t_made, b))
                used = held(eng, at(att_scores, b, 0))
                eng.wait_ge(max_t_made, value)
                if later(b):
                    eng.wait_ge(att_scores, used)
                row = q_stack[STACK:STACK + 1, :, :].rearrange("o h (j t) -> o (h j) t", t=P)
                eng.dma_start(row, max_t[:, :]).then_inc(max_row_in, 16)

            def store(b):
                value = held(eng, every(fin_made, b))
                eng.wait_ge(setup_dve, 1)
                eng.wait_ge(fin_made, value)
                eng.dma_start(out_v[b], fin[:, :, :]).then_inc(out_stored, 16)

            def prologue():
                load_x(0)
                eng.dma_start(ident[:, :], consts[:, 0:P]).then_inc(ident_in, 16)
                eng.dma_start(wa[:, :], w_attn).then_inc(wa_in, 16)
                eng.dma_start(consts_f, consts).then_inc(consts_in, 16)
                load_x(1)
                for dst, src in ((wp[:, :], w_proj), (gam[:, :], gamma), (wqs[:, :], wq.rearrange("k l d -> k (l d)")),
                                 (keyt[:, :], keys), (wdt[:, :], down),
                                 (wu[:, :, :], up.rearrange("(c p) d -> p c d", p=P))):
                    eng.dma_start(dst, src).then_inc(weights_in, 16)
                eng.wait_ge(setup_dve, 3)
                eng.dma_start(k_stack[STACK:STACK + 1, :], ones_row).then_inc(ones_in, 16)
                stack_pieces(0)
                load_residual(0)
                place_max_row(0)
                stack_pieces(1)

            def iteration(i, d, f, a, p):
                if p:
                    load_x(i + 2)
                if a:
                    load_residual(i + 1)
                    place_max_row(i + 1)
                if d:
                    store(i - 1)
                if p:
                    stack_pieces(i + 2)

            schedule(eng, prologue, iteration)
            eng.wait_ge(out_stored, every(out_stored, BATCHES - 1))

        @block.gpsimd
        def _(eng):
            def make_xhat(b):
                eng.wait_ge(ln1_step, every(ln1_step, b))
                if later(b):
                    eng.wait_ge(xhat_made, at(xhat_made, b, 0))
                eng.tensor_tensor(rstd1[:, :], ln_tmp[:, :], half_neg[:, :], ALU.pow).then_inc(rstd1_made, 1)
                if later(b):
                    eng.wait_ge(xhat_tp, at(xhat_tp, b, 0))
                eng.tensor_tensor(xhat[:, :, :], xin[:, :, :], mv1[:, :, 0:1].broadcast_to([P, TILES, D]),
                                  ALU.subtract).then_inc(x_centred, 1)
                eng.wait_ge(rstd1_made, every(rstd1_made, b))
                eng.wait_ge(x_centred, every(x_centred, b))
                eng.tensor_tensor(xhat[:, :, :], xhat[:, :, :], rstd1[:, :].unsqueeze(2).broadcast_to([P, TILES, D]),
                                  ALU.mult).then_inc(xhat_made, 1)

            def qk_low_piece(b):
                eng.wait_ge(qk_middle, every(qk_middle, b))
                if later(b):
                    eng.wait_ge(stack_in, at(stack_in, b, 0))
                    eng.wait_ge(scratch_in, at(scratch_in, b, 0))
                eng.tensor_tensor(qk_piece[:, 2, :], qk_rest[:, :], qk_piece[:, 1, :],
                                  ALU.subtract).then_inc(qk_low, 1)

            def scale(b):
                eng.wait_ge(ln2_step, every(ln2_step, b))
                if later(b):
                    eng.wait_ge(xn_made, at(xn_made, b, 0))
                eng.tensor_tensor(scale2[:, :], bounded[:, :], half_neg[:, :], ALU.pow).then_inc(scale2_made, 1)

            def sim_low_piece(b, j):
                eng.wait_ge(sim_high, at(sim_high, b, j + 1))
                if later(b):
                    eng.wait_ge(piece_tp, at(piece_tp, b, 0))
                v = sim[:, j, :].rearrange("p (h k) -> p h k", h=FH)
                eng.tensor_tensor(pieces[:, j, :, 1, :], v, pieces[:, j, :, 0, :],
                                  ALU.subtract).then_inc(sim_low, 1)

            def add_head(b, j, h):
                eng.wait_ge(prob_masked, at(prob_masked, b, j * FH + h + 1))
                if h == 1:
                    if later(b):
                        eng.wait_ge(acc_tp, at(acc_tp, b, 0))
                    so_far = prob[:, j * FH, :]
                else:
                    eng.wait_ge(acc_added, at(acc_added, b, j * (FH - 1) + h - 1))
                    so_far = acc[:, j, :]
                eng.tensor_tensor(acc[:, j, :], so_far, prob[:, j * FH + h, :], ALU.add).then_inc(acc_added, 1)

            def prologue():
                eng.memset(half_neg[:, :], -0.5).then_inc(setup_pool, 1)
                eng.memset(v_blocks[:, :, :], 0.0).then_inc(setup_pool, 1)
                eng.memset(one_blocks[:, :], 0.0).then_inc(setup_pool, 1)
                eng.memset(all_ones[:, :], 1.0).then_inc(setup_pool, 1)
                eng.wait_ge(setup_pool, 4)
                eng.memset(one_blocks[:, :].rearrange("p (m w) -> p m w", m=4)[:, :, 0:HD],
                           1.0).then_inc(setup_pool, 1)
                make_xhat(0)
                make_xhat(1)
                qk_low_piece(0)
                eng.wait_ge(unit_step, 3)
                eng.tensor_tensor(unit_inv[:, :], unit[:, :], half_neg[:, 0:1], ALU.pow).then_inc(unit_step, 1)
                qk_low_piece(1)
                scale(0)
                sim_low_piece(0, 0)
                sim_low_piece(0, 1)

            def iteration(i, d, f, a, p):
                if p:
                    make_xhat(i + 2)
                if f:
                    add_head(i, 0, 1)
                if p:
                    qk_low_piece(i + 2)
                if f:
                    for h in range(2, 6):
                        add_head(i, 0, h)
                if a:
                    scale(i + 1)
                if f:
                    add_head(i, 0, 6)
                    add_head(i, 0, 7)
                if f and a:
                    for h in range(1, 5):
                        add_head(i, 1, h)
                if a:
                    sim_low_piece(i + 1, 0)
                    sim_low_piece(i + 1, 1)
                if f and a:
                    for h in range(5, FH):
                        add_head(i, 1, h)

            schedule(eng, prologue, iteration)

        @block.scalar
        def _(eng):
            def xhat_back(b):
                eng.wait_ge(xhat_tp, every(xhat_tp, b))
                if later(b):
                    eng.wait_ge(v_made, at(v_made, b, 0))
                eng.activation(xhat_t[:, :], misc[0][:, 0:T], ACT.Copy).then_inc(xhat_t_made, 1)

            def qk_high_piece(b):
                eng.wait_ge(qk_made, every(qk_made, b))
                if later(b):
                    eng.wait_ge(stack_in, at(stack_in, b, 0))
                    eng.wait_ge(scratch_in, at(scratch_in, b, 0))
                eng.activation(qk_piece[:, 0, :], misc[1][:, :], ACT.Copy).then_inc(qk_high, 1)

            def qk_middle_piece(b):
                eng.wait_ge(qk_rest_made, every(qk_rest_made, b))
                eng.activation(qk_piece[:, 1, :], qk_rest[:, :], ACT.Copy).then_inc(qk_middle, 1)

            def v_back(b):
                eng.wait_ge(v_made, every(v_made, b))
                if later(b):
                    eng.wait_ge(v_copied, at(v_copied, b, 0))
                eng.activation(v_next[:, :, :], misc[0][:, 0:TILES * HD].rearrange("p (j e) -> p j e", e=HD),
                               ACT.Copy).then_inc(v_next_made, 1)

            def copy_v(b):
                if later(b):
                    eng.wait_ge(av_made, at(av_made, b, 0))
                else:
                    eng.wait_ge(setup_pool, 5)
                eng.wait_ge(v_next_made, every(v_next_made, b))
                eng.activation(v_blocks[:, :, :].rearrange("p j (m w) -> p j m w", m=4)[:, :, :, 0:HD],
                               v_next[:, :, :].unsqueeze(2).broadcast_to([P, TILES, 4, HD]),
                               ACT.Copy).then_inc(v_copied, 1)

            def max_scores_back(b, u):
                eng.wait_ge(max_scores, at(max_scores, b, u + 1))
                if u == 0 and later(b):
                    eng.wait_ge(max_step, at(max_step, b, 0))
                if u < 4:
                    dst = halves[0][:, 4 * u:4 * u + 4, 0, :]
                    src = att[u % 2][:, :].rearrange("p (h k) -> p h k", h=4)
                else:
                    dst = late_scores[:, 2 * (u - 4):2 * (u - 3), :].rearrange("p h k -> p (h k)")
                    src = att[u % 2][:, :]
                eng.activation(dst, src, ACT.Copy).then_inc(max_kept, 1)

            def max_back(b):
                eng.wait_ge(max_tp, every(max_tp, b))
                if later(b):
                    eng.wait_ge(max_row_in, at(max_row_in, b, 0))
                eng.activation(max_t[:, :], misc[0][0:H * TILES, 0:P], ACT.Copy).then_inc(max_t_made, 1)

            def att_exp(b, u):
                if u == 0 and later(b):
                    eng.wait_ge(av_made, at(av_made, b, 0))
                eng.wait_ge(att_scores, at(att_scores, b, u + 1))
                if u < 8:
                    dst = probs0[:, 2 * u:2 * u + 2, :].rearrange("p h t -> p (h t)")
                else:
                    dst = probs1[:, 4 * (u - 8):4 * (u - 7), :].rearrange("p h t -> p (h t)")
                eng.activation(dst, att[u % 2][:, :], ACT.Exp, scale=float(HD) ** -0.5).then_inc(att_probs, 1)

            def copy_x2(b):
                eng.wait_ge(x2_made, every(x2_made, b))
                if later(b):
                    eng.wait_ge(fin_made, at(fin_made, b, 0))
                eng.activation(x2_kept[:, :, :], x2[:, :, :], ACT.Copy).then_inc(x2_copied, 1)

            def xn_back(b):
                eng.wait_ge(xn_tp, every(xn_tp, b))
                if later(b):
                    eng.wait_ge(hidden, at(hidden, b, 0))
                    eng.wait_ge(sim_made, at(sim_made, b, 0))
                eng.activation(xn_t[:, :], misc[0][:, 0:T], ACT.Copy).then_inc(xn_t_made, 1)

            def sim_back(b, j):
                eng.wait_ge(sim_made, at(sim_made, b, j + 1))
                if later(b):
                    eng.wait_ge(select_step, at(select_step, b, 0))
                    eng.wait_ge(sim_low, at(sim_low, b, 0))
                eng.activation(sim[:, j, :], misc[1 - j][:, :], ACT.Copy).then_inc(sim_kept, 1)

            def sim_high_piece(b, j):
                eng.wait_ge(sim_kept, at(sim_kept, b, j + 1))
                if later(b):
                    eng.wait_ge(piece_tp, at(piece_tp, b, 0))
                v = sim[:, j, :].rearrange("p (h k) -> p h k", h=FH)
                eng.activation(pieces[:, j, :, 0, :], v, ACT.Copy).then_inc(sim_high, 1)

            def pieces_back(b, j):
                eng.wait_ge(piece_tp, at(piece_tp, b, j + 1))
                if later(b):
                    eng.wait_ge(scores_made, at(scores_made, b, 0))
                eng.activation(pieces_t[:, j, :, :].rearrange("p h t -> p (h t)"),
                               misc[j][:, :].bitcast(FP16), ACT.Copy).then_inc(piece_t_made, 1)

            def activate(b, n):
                eng.wait_ge(hidden, at(hidden, b, n + 1))
                if later(b):
                    eng.wait_ge(gated, at(gated, b, 0))
                eng.activation(act_t[:, 4 * n:4 * n + 4, :].rearrange("p c t -> p (c t)"),
                               score[n][:, :], ACT.Gelu).then_inc(act_made, 1)

            def best_exp(b, j):
                eng.wait_ge(shifted_made, at(shifted_made, b, j + 1))
                if not later(b):
                    eng.wait_ge(unit_step, 6)
                eng.activation(exps[:, j, :, :].rearrange("p h k -> p (h k)"),
                               shifted[:, j, :, :].rearrange("p h k -> p (h k)"), ACT.Exp,
                               scale=unit[:, :]).then_inc(exps_made, 1)

            def log_sum(b, j):
                eng.wait_ge(total_made, at(total_made, b, j + 1))
                eng.activation(log_total[:, j, :], total[:, j, :], ACT.Ln).then_inc(log_made, 1)

            def threshold(b, j):
                eng.wait_ge(cut_arg_made, at(cut_arg_made, b, j + 1))
                eng.activation(cut_prob[:, j, :], cut_arg[:, j, :], ACT.Exp).then_inc(cut_prob_made, 1)

            def pair_probs(b, j, h):
                g = j * FH + h
                eng.wait_ge(scores_made, at(scores_made, b, g + 1))
                if later(b):
                    eng.wait_ge(acc_added, at(acc_added, b - 1, j * (FH - 1) + max(h, 1)))
                elif g == 0:
                    eng.wait_ge(setup_dve, 3)
                    eng.wait_ge(norms_made, 1)
                eng.activation(prob[:, g, :], score[g % 2][:, :], ACT.Exp, bias=neg_lse[:, j, h:h + 1],
                               scale=unit[:, :]).then_inc(prob_made, 1)

            def prologue():
                xhat_back(0)
                qk_high_piece(0)
                v_back(0)
                copy_v(0)
                qk_middle_piece(0)
                xhat_back(1)
                for u in range(MAX_STEPS):
                    max_scores_back(0, u)
                max_back(0)
                for u in range(MAX_STEPS):
                    att_exp(0, u)
                qk_high_piece(1)
                v_back(1)
                qk_middle_piece(1)
                xn_back(0)
                sim_back(0, 0)
                sim_back(0, 1)
                sim_high_piece(0, 0)
                sim_high_piece(0, 1)

            def iteration(i, d, f, a, p):
                if a:
                    copy_v(i + 1)
                    for u in range(MAX_STEPS):
                        max_scores_back(i + 1, u)
                if f:
                    best_exp(i, 0)
                    log_sum(i, 0)
                    pieces_back(i, 0)
                    pieces_back(i, 1)
                if a:
                    max_back(i + 1)
                if f:
                    activate(i, 0)
                    activate(i, 1)
                    threshold(i, 0)
                if a:
                    for u in range(4):
                        att_exp(i + 1, u)
                if p:
                    xhat_back(i + 2)
                if a:
                    att_exp(i + 1, 4)
                    att_exp(i + 1, 5)
                if f:
                    pair_probs(i, 0, 0)
                if a:
                    att_exp(i + 1, 6)
                    att_exp(i + 1, 7)
                if f:
                    pair_probs(i, 0, 1)
                if a:
                    att_exp(i + 1, 8)
                    att_exp(i + 1, 9)
                if p:
                    qk_high_piece(i + 2)
                    v_back(i + 2)
                if f:
                    best_exp(i, 1)
                if a:
                    att_exp(i + 1, 10)
                    att_exp(i + 1, 11)
                if f:
                    pair_probs(i, 0, 2)
                    pair_probs(i, 0, 3)
                if p:
                    qk_middle_piece(i + 2)
                if f:
                    for h in range(4, FH):
                        pair_probs(i, 0, h)
                    log_sum(i, 1)
                    copy_x2(i)
                    threshold(i, 1)
                    for h in range(3):
                        pair_probs(i, 1, h)
                    pair_probs(i, 1, 3)
                if a:
                    xn_back(i + 1)
                if f:
                    pair_probs(i, 1, 4)
                if a:
                    sim_back(i + 1, 0)
                if f:
                    for h in range(5, FH):
                        pair_probs(i, 1, h)
                if a:
                    sim_back(i + 1, 1)
                    sim_high_piece(i + 1, 0)
                    sim_high_piece(i + 1, 1)

            schedule(eng, prologue, iteration)

        @block.vector
        def _(eng):

            def ln1(b):
                eng.wait_ge(x_in, every(x_in, b))
                for j in range(TILES):
                    eng.bn_stats(stat1[:, j, :], xin[:, j, :]).then_inc(ln1_step, 1)
                value = held(eng, at(ln1_step, b, TILES))
                if later(b):
                    eng.wait_ge(setup_dve, 1)
                eng.wait_ge(ln1_step, value)
                for j in range(TILES):
                    eng.bn_aggr(mv1[:, j, :], stat1[:, j, :]).then_inc(ln1_step, 1)
                eng.wait_ge(ln1_step, at(ln1_step, b, 2 * TILES))
                if later(b):
                    eng.wait_ge(rstd1_made, at(rstd1_made, b, 0))
                eng.tensor_scalar(ln_tmp[:, :], mv1[:, :, 1], LN_EPS, None, ALU.add).then_inc(ln1_step, 1)

            def qk_remainder(b):
                eng.wait_ge(qk_high, every(qk_high, b))
                eng.wait_ge(qk_made, every(qk_made, b))
                if later(b):
                    eng.wait_ge(qk_low, at(qk_low, b, 0))
                eng.tensor_tensor(qk_rest[:, :], misc[1][:, :], qk_piece[:, 0, :],
                                  ALU.subtract).then_inc(qk_rest_made, 1)

            def fold_max(b, first, last):
                if first == 0:
                    eng.wait_ge(max_kept, every(max_kept, b))
                    eng.tensor_tensor(halves[0][:, :, 1, :], late_scores[:, :, 0:P], late_scores[:, :, P:T],
                                      ALU.max).then_inc(max_step, 1)
                for n in range(max(first, 1), min(last, 5)):
                    eng.wait_ge(max_step, at(max_step, b, n))
                    wide = halves[n - 1][:, :, :, :].rearrange("p h j k -> p (h j) k")
                    half = wide.shape[2] // 2
                    eng.tensor_tensor(halves[n][:, :, :, :].rearrange("p h j k -> p (h j) k"), wide[:, :, 0:half],
                                      wide[:, :, half:2 * half], ALU.max).then_inc(max_step, 1)
                if last < 6:
                    return
                eng.wait_ge(max_step, at(max_step, b, 5))
                if later(b):
                    eng.wait_ge(max_tp, at(max_tp, b, 0))
                eng.tensor_reduce(neg_max[:, :, :], halves[4][:, :, :, :], AX.X, ALU.max,
                                  negate=True).then_inc(max_step, 1)

            def make_y(b):
                if later(b):
                    eng.wait_ge(proj_made, at(proj_made, b, 0))
                eng.wait_ge(av_made, every(av_made, b))
                eng.reciprocal(y_t[:, :], misc[0][:, T:2 * T]).then_inc(y_inverse, 1)
                eng.wait_ge(y_inverse, every(y_inverse, b))
                eng.tensor_tensor(y_t[:, :], misc[0][:, 0:T], y_t[:, :], ALU.mult).then_inc(y_t_made, 1)

            def make_x2(b):
                eng.wait_ge(proj_made, every(proj_made, b))
                eng.wait_ge(xres_in, every(xres_in, b))
                if later(b):
                    eng.wait_ge(x2_copied, at(x2_copied, b, 0))
                if later(b):
                    eng.wait_ge(xn_made, at(xn_made, b, 0))
                eng.tensor_tensor(x2[:, :, :].rearrange("p j d -> p (j d)"),
                                  xres[:, :, :].rearrange("p j d -> p (j d)"),
                                  att[1][:, 0:TILES * D], ALU.add).then_inc(x2_made, 1)
                eng.wait_ge(x2_made, every(x2_made, b))
                if later(b):
                    eng.wait_ge(scale2_made, at(scale2_made, b, 0))
                for j in range(TILES):
                    eng.bn_stats(stat2[:, j, :], x2[:, j, :]).then_inc(ln2_step, 1)
                value = held(eng, at(ln2_step, b, TILES))
                eng.wait_ge(setup_dve, 1)
                eng.wait_ge(ln2_step, value)
                for j in range(TILES):
                    eng.bn_aggr(mv2[:, j, :], stat2[:, j, :]).then_inc(ln2_step, 1)
                eng.wait_ge(ln2_step, at(ln2_step, b, 2 * TILES))
                eng.tensor_scalar(bounded[:, :], mv2[:, :, 1], LN_EPS, 1e-24 / D, ALU.add,
                                  ALU.mult).then_inc(ln2_step, 1)
                eng.wait_ge(ln2_step, at(ln2_step, b, 2 * TILES + 1))
                eng.tensor_tensor(bounded[:, :], mv2[:, :, 1], bounded[:, :], ALU.max).then_inc(ln2_step, 1)

            def make_xn(b):
                eng.wait_ge(scale2_made, every(scale2_made, b))
                eng.wait_ge(ln2_step, every(ln2_step, b))
                if later(b):
                    eng.wait_ge(xn_tp, at(xn_tp, b, 0))
                for j in range(TILES):
                    eng.tensor_scalar(xn[:, j, :], x2[:, j, :], mv2[:, j, 0:1], scale2[:, j:j + 1],
                                      ALU.subtract, ALU.mult).then_inc(xn_made, 1)

            def select_keys(b, j):
                n = j * SELECT
                keys_of = [sim[:, j, l * KEYS:(l + 1) * KEYS] for l in range(LISTS)]
                value = held(eng, at(sim_kept, b, j + 1))
                eng.wait_ge(setup_dve, 1)
                eng.wait_ge(sim_kept, value)
                for l in range(LISTS):
                    eng.max(top[:, l, 0:8], keys_of[l]).then_inc(select_step, 1)
                for half in range(2):
                    value = held(eng, at(select_step, b, n + (half + 1) * LISTS // 2))
                    eng.wait_ge(setup_dve, 1)
                    eng.wait_ge(select_step, value)
                    for l in range(half * LISTS // 2, (half + 1) * LISTS // 2):
                        eng.match_replace(left[:, l, :], top[:, l, 0:8], keys_of[l], LOWEST).then_inc(select_step, 1)
                n += LISTS
                for half in range(2):
                    value = held(eng, at(select_step, b, n + (half + 1) * LISTS // 2))
                    eng.wait_ge(setup_dve, 1)
                    eng.wait_ge(select_step, value)
                    for l in range(half * LISTS // 2, (half + 1) * LISTS // 2):
                        eng.max(top[:, l, 8:16], left[:, l, :]).then_inc(select_step, 1)
                n += 2 * LISTS
                col = 0
                for a0, na, nb in PAIR_BLOCKS:
                    if a0 + na > 8 or nb > 8:
                        eng.wait_ge(select_step, at(select_step, b, n))
                    dst = cand[:, :, col:col + na * nb].rearrange("p h (a b) -> p h a b", b=nb)
                    xs = top[:, 0:LISTS:2, a0:a0 + na].unsqueeze(3).broadcast_to([P, FH, na, nb])
                    ys = top[:, 1:LISTS:2, 0:nb].unsqueeze(2).broadcast_to([P, FH, na, nb])
                    eng.tensor_tensor(dst, xs, ys, ALU.add).then_inc(select_step, 1)
                    col += na * nb
                ends = top[:, :, 0:TOPK:TOPK - 1].rearrange("p (h a) e -> p h a e", a=2)
                eng.tensor_reduce(size[:, j, :], ends, AX.XY, ALU.add,
                                  apply_absolute_value=True).then_inc(select_step, 1)

            def select_pairs(b, j):
                n = j * SELECT + 3 * LISTS + len(PAIR_BLOCKS)
                value = held(eng, at(select_step, b, n))
                eng.wait_ge(setup_dve, 1)
                eng.wait_ge(select_step, value)
                n += 1
                for h in range(FH):
                    eng.max(best[:, j, h, 0:8], cand[:, h, :]).then_inc(select_step, 1)
                for half in range(2):
                    value = held(eng, at(select_step, b, n + (half + 1) * FH // 2))
                    eng.wait_ge(setup_dve, 1)
                    eng.wait_ge(select_step, value)
                    for h in range(half * FH // 2, (half + 1) * FH // 2):
                        eng.match_replace(cand_left[:, h, :], best[:, j, h, 0:8], cand[:, h, :],
                                          LOWEST).then_inc(select_step, 1)
                n += FH
                for half in range(2):
                    value = held(eng, at(select_step, b, n + (half + 1) * FH // 2))
                    eng.wait_ge(setup_dve, 1)
                    eng.wait_ge(select_step, value)
                    for h in range(half * FH // 2, (half + 1) * FH // 2):
                        eng.max(best[:, j, h, 8:16], cand_left[:, h, :]).then_inc(select_step, 1)
                n += 2 * FH
                eng.wait_ge(select_step, at(select_step, b, n))
                eng.tensor_tensor(shifted[:, j, :, :], best[:, j, :, :],
                                  best[:, j, :, 0:1].broadcast_to([P, FH, TOPK]),
                                  ALU.subtract).then_inc(shifted_made, 1)
                eng.scalar_tensor_tensor(cut[:, j, :], size[:, j, :], -float(2 ** -21), best[:, j, :, TOPK - 1],
                                         ALU.mult, ALU.add).then_inc(select_step, 1)

            def sum_best(b, j):
                eng.wait_ge(exps_made, at(exps_made, b, j + 1))
                eng.tensor_reduce(total[:, j, :], exps[:, j, :, :], AX.X, ALU.add).then_inc(total_made, 1)

            def log_sum_exp(b, j):
                if later(b):
                    eng.wait_ge(prob_made, at(prob_made, b, 0))
                eng.wait_ge(log_made, at(log_made, b, j + 1))
                eng.scalar_tensor_tensor(neg_lse[:, j, :], best[:, j, :, 0], neg_unit[:, :],
                                         log_total[:, j, :], ALU.mult, ALU.subtract).then_inc(lse_step, 1)
                eng.wait_ge(select_step, at(select_step, b, (j + 1) * SELECT))
                eng.wait_ge(lse_step, at(lse_step, b, j + 1))
                eng.scalar_tensor_tensor(cut_arg[:, j, :], cut[:, j, :], unit[:, :],
                                         neg_lse[:, j, :], ALU.mult, ALU.add).then_inc(cut_arg_made, 1)

            def mask(b, j, h):
                g = j * FH + h
                if h == 0:
                    eng.wait_ge(cut_prob_made, at(cut_prob_made, b, j + 1))
                eng.wait_ge(prob_made, at(prob_made, b, g + 1))
                eng.scalar_tensor_tensor(prob[:, g, :], prob[:, g, :], cut_prob[:, j, h:h + 1], prob[:, g, :],
                                         ALU.is_ge, ALU.mult).then_inc(prob_masked, 1)

            def add_late_head(h):
                g = FH + h
                eng.wait_ge(prob_masked, at(prob_masked, BATCHES - 1, g + 1))
                if h == 1:
                    eng.wait_ge(acc_tp, at(acc_tp, BATCHES - 1, 0))
                else:
                    eng.wait_ge(late_added, h - 1)
                so_far = prob[:, FH, :] if h == 1 else acc[:, 1, :]
                eng.tensor_tensor(acc[:, 1, :], so_far, prob[:, g, :], ALU.add).then_inc(late_added, 1)

            def gate(b, j):
                eng.wait_ge(act_made, every(act_made, b))
                if later(b):
                    eng.wait_ge(down_made, at(down_made, b, 0))
                eng.wait_ge(acc_tp, at(acc_tp, b, j + 1))
                toks = slice(j * P, (j + 1) * P)
                eng.tensor_tensor(gated_t[:, :, toks], score[j][:, :].rearrange("p (c t) -> p c t", t=P),
                                  act_t[:, :, toks], ALU.mult).then_inc(gated, 1)

            def finish(b):
                eng.wait_ge(down_made, every(down_made, b))
                eng.wait_ge(x2_copied, every(x2_copied, b))
                if later(b):
                    eng.wait_ge(out_stored, at(out_stored, b, 0))
                eng.tensor_tensor(fin[:, :, :].rearrange("p j d -> p (j d)"),
                                  x2_kept[:, :, :].rearrange("p j d -> p (j d)"),
                                  misc[1][:, 0:TILES * D], ALU.add).then_inc(fin_made, 1)

            def prologue():
                ln1(0)
                eng.wait_ge(consts_in, 16)
                eng.tensor_copy(cb[:, :], consts_f[:, 0:SEL]).then_inc(setup_dve, 1)
                eng.tensor_copy(ident_h[:, :], consts_f[:, 0:P]).then_inc(setup_dve, 1)
                eng.tensor_copy(sel[:, :], consts_f[:, SEL:SEL + EXPERTS]).then_inc(setup_dve, 1)
                qk_remainder(0)
                ln1(1)
                eng.wait_ge(wkey_made, 1)
                eng.tensor_scalar(wkey[:, :], score[0][:, BANK:2 * BANK], gam[:, 0:1], None,
                                  ALU.mult).then_inc(wkey_read, 1)
                eng.wait_ge(wkey_read, 1)
                eng.tensor_tensor(wkey_sq[:, :], wkey[:, :], wkey[:, :], ALU.mult).then_inc(unit_step, 1)
                eng.wait_ge(weights_in, 6 * 16)
                eng.tensor_scalar(wdt[:, :], wdt[:, :], gam[:, 0:1], None, ALU.mult).then_inc(setup_done, 1)
                eng.wait_ge(norms_made, 1)
                eng.tensor_reduce(unit[:, :], score[0][:, 0:BANK], AX.X, ALU.max).then_inc(unit_step, 1)
                eng.wait_ge(unit_step, 2)
                eng.tensor_scalar(unit[:, :], unit[:, :], 1e-30, D / SIM_PEAK ** 2, ALU.max,
                                  ALU.mult).then_inc(unit_step, 1)
                eng.wait_ge(unit_step, 4)
                eng.tensor_scalar(wkey[:, :], wkey[:, :], unit_inv[:, :], None, ALU.mult).then_inc(setup_done, 1)
                eng.reciprocal(unit[:, :], unit_inv[:, :]).then_inc(unit_step, 1)
                eng.wait_ge(unit_step, 5)
                eng.tensor_scalar(neg_unit[:, :], unit[:, :], -1.0, None, ALU.mult).then_inc(unit_step, 1)
                fold_max(0, 0, 6)
                qk_remainder(1)
                make_y(0)
                make_x2(0)
                make_xn(0)

            def iteration(i, d, f, a, p):
                if f:
                    select_keys(i, 0)
                    select_pairs(i, 0)
                if a:
                    fold_max(i + 1, 0, 1)
                if f:
                    sum_best(i, 0)
                if d:
                    gate(i - 1, 0)
                if a:
                    fold_max(i + 1, 1, 6)
                if d:
                    gate(i - 1, 1)
                if p:
                    ln1(i + 2)
                if f:
                    log_sum_exp(i, 0)
                    select_keys(i, 1)
                    select_pairs(i, 1)
                if d:
                    finish(i - 1)
                if f:
                    mask(i, 0, 0)
                    mask(i, 0, 1)
                if p:
                    qk_remainder(i + 2)
                if f:
                    sum_best(i, 1)
                    for h in range(2, FH):
                        mask(i, 0, h)
                    log_sum_exp(i, 1)
                if a:
                    make_y(i + 1)
                if f:
                    mask(i, 1, 0)
                if a:
                    make_x2(i + 1)
                if f:
                    mask(i, 1, 1)
                if a:
                    make_xn(i + 1)
                if f:
                    if not a:
                        add_late_head(1)
                    for h in range(2, FH):
                        mask(i, 1, h)
                        if not a:
                            add_late_head(h)

            schedule(eng, prologue, iteration)

        @block.tensor
        def _(eng):
            def fold_keys():
                eng.wait_ge(weights_in, 6 * 16)
                for l in range(LISTS):
                    ins = eng.matmul(score[0][:, BANK + l * KEYS:BANK + (l + 1) * KEYS], wqs[:, l * D:(l + 1) * D],
                                     keyt[:, l * KEYS:(l + 1) * KEYS], start=True, stop=True)
                ins.then_inc(wkey_made, 1)

            def two_transposes(bank, src, sig):
                for j in range(TILES):
                    ins = eng.transpose(bank[:, j * P:(j + 1) * P], src[:, j, :], ident[:, :])
                ins.then_inc(sig, 1)

            def xhat_transpose(b, reader, of_batch):
                eng.wait_ge(xhat_made, every(xhat_made, b))
                eng.wait_ge(reader, every(reader, of_batch))
                two_transposes(misc[0], xhat, xhat_tp)

            def project_qkv(b, reader, of_batch):
                eng.wait_ge(xhat_t_made, every(xhat_t_made, b))
                eng.wait_ge(reader, every(reader, of_batch))
                eng.matmul(misc[1][:, 0:T], wa[:, 0:D], xhat_t[:, :], start=True, stop=True)
                eng.matmul(misc[1][:, T:2 * T], wa[:, 2 * HD:D + 2 * HD], xhat_t[:, :],
                           start=True, stop=True).then_inc(qk_made, 1)
                for j in range(TILES):
                    ins = eng.matmul(misc[0][:, j * HD:(j + 1) * HD], xhat_t[:, j * P:(j + 1) * P],
                                     wa[:, D + HD:D + 2 * HD], start=True, stop=True)
                ins.then_inc(v_made, 1)

            def scores_for_max(b, u):
                if u == 0:
                    if later(b):
                        eng.wait_ge(att_probs, at(att_probs, b, 0))
                    eng.wait_ge(stack_in, every(stack_in, b))
                elif u == 1:
                    if later(b):
                        eng.wait_ge(x2_made, at(x2_made, b, 0))
                else:
                    eng.wait_ge(max_kept, at(max_kept, b, u - 1))
                bank = att[u % 2]
                nh, nk, h0, j = (4, P, 4 * u, 0) if u < 4 else (2, T, 2 * (u - 4), 1)
                for n in range(nh):
                    eng.matmul(bank[:, n * nk:(n + 1) * nk], q_stack[0:STACK, h0 + n, j * P:(j + 1) * P],
                               k_stack[0:STACK, 0:nk], start=n == 0, stop=False)
                late = bank[:, :].rearrange("p (n k) -> p n k", k=nk)[:, :, nk - P:nk]
                ins = eng.matmul(late, ident_bf, mask_q[:, 0:nh, :], start=False, stop=True)
                ins.then_inc(max_scores, 1)

            def max_transpose(b):
                eng.wait_ge(max_step, every(max_step, b))
                if later(b):
                    eng.wait_ge(piece_t_made, at(piece_t_made, b - 1, 1))
                else:
                    eng.wait_ge(xhat_t_made, at(xhat_t_made, b + 1, 1))
                eng.transpose(misc[0][0:H * TILES, 0:P], neg_max[:, :, :].rearrange("p h j -> p (h j)"),
                              ident[:, :]).then_inc(max_tp, 1)

            def scores_for_probs(b, u):
                if u == 0:
                    eng.wait_ge(max_row_in, every(max_row_in, b))
                    if not later(b):
                        eng.wait_ge(ones_in, 16)
                if u < 2:
                    eng.wait_ge(max_kept, every(max_kept, b))
                else:
                    eng.wait_ge(att_probs, at(att_probs, b, u - 1))
                bank = att[u % 2]
                if u < 8:
                    nq, k, q = T, k_stack[:, 0:P], q_stack[:, 2 * u:2 * u + 2, :]
                else:
                    nq, k, q = P, k_stack[:, P:T], q_stack[:, 4 * (u - 8):4 * (u - 7), P:T]
                eng.matmul(bank[:, :], k, q, start=True, stop=False)
                early = bank[:, :].rearrange("p (n t) -> p n t", t=nq)[:, :, 0:P]
                eng.matmul(early, ident_bf, mask_t[:, 0:BANK // nq, :], start=False, stop=True).then_inc(att_scores, 1)

            def weigh_values(b, j, heads, reader, of_batch):
                if j == 0:
                    eng.wait_ge(v_copied, every(v_copied, b))
                    eng.wait_ge(reader, every(reader, of_batch))
                    eng.wait_ge(att_probs, at(att_probs, b, 8))
                else:
                    eng.wait_ge(att_probs, every(att_probs, b))
                for m in heads:
                    for n in range(2):
                        for g in range(4):
                            block = (one_blocks[:, :] if n else v_blocks[:, j, :])[:, 32 * m:32 * m + 32]
                            rows = misc[0][32 * g:32 * g + 32, n * T:(n + 1) * T]
                            if j == 0:
                                eng.matmul(rows, block, probs0[:, 4 * g + m, :], start=m + n == 0, stop=False)
                            else:
                                ins = eng.matmul(rows[:, P:T], block, probs1[:, 4 * g + m, :], start=False,
                                                 stop=m + n == 4)
                if j == 1:
                    ins.then_inc(av_made, 1)

            def project_y(b):
                eng.wait_ge(y_t_made, every(y_t_made, b))
                for j in range(TILES):
                    ins = eng.matmul(att[1][:, j * D:(j + 1) * D], y_t[:, j * P:(j + 1) * P], wp[:, :],
                                     start=True, stop=True)
                ins.then_inc(proj_made, 1)

            def xn_transpose(b, reader, of_batch):
                eng.wait_ge(xn_made, every(xn_made, b))
                eng.wait_ge(reader, every(reader, of_batch))
                two_transposes(misc[0], xn, xn_tp)

            def key_scores(b, j, reader, of_batch):
                eng.wait_ge(reader, every(reader, of_batch))
                eng.wait_ge(xn_t_made, every(xn_t_made, b))
                eng.matmul(misc[1 - j][:, :], xn_t[:, j * P:(j + 1) * P], wkey[:, :],
                           start=True, stop=True).then_inc(sim_made, 1)

            def hidden_chunks(b, n):
                if later(b):
                    eng.wait_ge(gated, at(gated, b - 1, n + 1))
                for c in range(4 * n, 4 * n + 4):
                    ins = eng.matmul(score[n][:, (c % 4) * T:(c % 4 + 1) * T], wdt[:, c * P:(c + 1) * P],
                                     xn_t[:, :], start=True, stop=True)
                ins.then_inc(hidden, 1)

            def piece_transposes(b, j):
                eng.wait_ge(sim_kept, every(sim_kept, b))
                eng.wait_ge(sim_low, at(sim_low, b, j + 1))
                dst = misc[j][:, :].bitcast(FP16)
                for h in range(FH):
                    ins = eng.transpose(dst[:, h * P:(h + 1) * P],
                                        pieces[:, j, h, :, :].rearrange("p s k -> p (s k)"), ident_h[:, :])
                ins.then_inc(piece_tp, 1)

            def pair_scores(b, j, h):
                g = j * FH + h
                if h == 0:
                    eng.wait_ge(piece_t_made, at(piece_t_made, b, j + 1))
                if g < 2:
                    eng.wait_ge(act_made, at(act_made, b, g + 1))
                else:
                    eng.wait_ge(prob_made, at(prob_made, b, g - 1))
                for half in range(2):
                    cols = slice(half * BANK, (half + 1) * BANK)
                    ins = eng.matmul(score[g % 2][:, cols], pieces_t[:, j, h, :], sel[:, cols],
                                     start=True, stop=True)
                ins.then_inc(scores_made, 1)

            def acc_transposes(b, j):
                eng.wait_ge(prob_made, at(prob_made, b, TILES * FH - 1 + j))
                if j == 1 and isinstance(b, int) and b == BATCHES - 1:
                    eng.wait_ge(late_added, FH - 1)
                else:
                    eng.wait_ge(acc_added, at(acc_added, b, (FH - 1) * (j + 1)))
                for c in range(CH):
                    ins = eng.transpose(score[j][:, c * P:(c + 1) * P], acc[:, j, c * P:(c + 1) * P], ident[:, :])
                ins.then_inc(acc_tp, 1)

            def expert_output(b, j, of_batch):
                eng.wait_ge(piece_t_made, every(piece_t_made, of_batch))
                eng.wait_ge(gated, at(gated, b, j + 1))
                for c in range(CH):
                    ins = eng.matmul(misc[1][:, j * D:(j + 1) * D], gated_t[:, c, j * P:(j + 1) * P],
                                     wu[:, c, :], start=c == 0, stop=c == CH - 1)
                ins.then_inc(down_made, 1)

            def prologue():
                eng.wait_ge(ident_in, 16)
                xhat_transpose(0, setup_pool, 0)
                eng.wait_ge(wa_in, 16)
                project_qkv(0, xhat_t_made, 0)
                fold_keys()
                xhat_transpose(1, v_next_made, 0)
                eng.wait_ge(unit_step, 1)
                eng.matmul(score[0][:, 0:BANK], all_ones[:, :], wkey_sq[:, :], start=True,
                           stop=True).then_inc(norms_made, 1)
                eng.wait_ge(setup_dve, 3)
                for u in range(MAX_STEPS):
                    scores_for_max(0, u)
                max_transpose(0)
                for u in range(MAX_STEPS):
                    scores_for_probs(0, u)
                project_qkv(1, qk_rest_made, 0)
                weigh_values(0, 0, range(4), v_next_made, 1)
                weigh_values(0, 1, range(4), v_next_made, 1)
                project_y(0)
                eng.wait_ge(setup_done, 2)
                xn_transpose(0, v_next_made, 1)
                key_scores(0, 0, qk_rest_made, 1)
                key_scores(0, 1, qk_rest_made, 1)

            def iteration(i, d, f, a, p):
                if a:
                    for u in range(MAX_STEPS):
                        scores_for_max(i + 1, u)
                if d:
                    acc_transposes(i - 1, 0)
                if f:
                    piece_transposes(i, 0)
                    piece_transposes(i, 1)
                if d:
                    acc_transposes(i - 1, 1)
                if f:
                    hidden_chunks(i, 0)
                if a:
                    max_transpose(i + 1)
                if f:
                    hidden_chunks(i, 1)
                if d:
                    expert_output(i - 1, 0, i if f else i - 1)
                if a:
                    for u in range(4):
                        scores_for_probs(i + 1, u)
                if p:
                    xhat_transpose(i + 2, max_t_made, i + 1)
                if a:
                    scores_for_probs(i + 1, 4)
                    scores_for_probs(i + 1, 5)
                if f:
                    pair_scores(i, 0, 0)
                if a:
                    scores_for_probs(i + 1, 6)
                    scores_for_probs(i + 1, 7)
                if f:
                    pair_scores(i, 0, 1)
                if d:
                    expert_output(i - 1, 1, i if f else i - 1)
                if a:
                    scores_for_probs(i + 1, 8)
                    scores_for_probs(i + 1, 9)
                if p:
                    project_qkv(i + 2, fin_made if d else piece_t_made, i - 1 if d else i)
                if f:
                    pair_scores(i, 0, 2)
                if a:
                    scores_for_probs(i + 1, 10)
                    scores_for_probs(i + 1, 11)
                if f:
                    pair_scores(i, 0, 3)
                    for m in range(4):
                        if a:
                            weigh_values(i + 1, 0, [m], v_next_made if p else max_t_made, i + 2 if p else i + 1)
                        pair_scores(i, 0, 4 + m)
                if a:
                    weigh_values(i + 1, 1, range(4), v_next_made if p else max_t_made, i + 2 if p else i + 1)
                if f:
                    pair_scores(i, 1, 0)
                    pair_scores(i, 1, 1)
                if a:
                    project_y(i + 1)
                if f:
                    pair_scores(i, 1, 2)
                    pair_scores(i, 1, 3)
                if a:
                    xn_transpose(i + 1, y_t_made, i + 1)
                if f:
                    pair_scores(i, 1, 4)
                if a:
                    key_scores(i + 1, 0, qk_rest_made if p else fin_made, i + 2 if p else i - 1)
                if f:
                    pair_scores(i, 1, 5)
                if a:
                    key_scores(i + 1, 1, qk_rest_made if p else fin_made, i + 2 if p else i - 1)
                if f:
                    pair_scores(i, 1, 6)
                    pair_scores(i, 1, 7)

            schedule(eng, prologue, iteration)


def constants():
    import numpy as np
    eye = np.eye(P, dtype=np.float32)
    q, k = np.arange(P)[:, None], np.arange(P)[None, :]
    tri = np.where(k > q, np.float32(MASKED), np.float32(0))
    masks = [np.tile(tri, (1, 4)), np.tile(tri.T, (1, 4))]
    pair = np.arange(EXPERTS)
    spread = np.concatenate([(np.arange(KEYS)[:, None] == pair // KEYS),
                             (np.arange(KEYS)[:, None] == pair % KEYS)]).astype(np.float32)
    return np.hstack([eye] + masks + [np.ones((P, T), np.float32), np.vstack([spread, spread])])


def kernel(L0_attn_x, L0_attn_w_attn, L0_attn_w_proj, L0_ffn_gamma, L0_ffn_wq, L0_ffn_keys,
           L0_ffn_table_down, L0_ffn_table_up):
    import numpy as np
    import concourse.bacc as bacc
    from concourse.bass_utils import run_bass_kernel_spmd

    arrays = {
        "x": np.asarray(L0_attn_x),
        "w_attn": np.asarray(L0_attn_w_attn),
        "w_proj": np.asarray(L0_attn_w_proj),
        "gamma": np.asarray(L0_ffn_gamma).reshape(D, 1),
        "wq": np.asarray(L0_ffn_wq).reshape(2, FH, DK, D).transpose(2, 1, 0, 3).reshape(DK, LISTS, D),
        "keys": np.asarray(L0_ffn_keys).transpose(3, 0, 2, 1).reshape(DK, LISTS * KEYS),
        "down": np.asarray(L0_ffn_table_down)[:EXPERTS].T,
        "up": np.asarray(L0_ffn_table_up)[:EXPERTS],
        "consts": constants(),
    }
    arrays = {n: np.ascontiguousarray(a) for n, a in arrays.items()}
    nc = bacc.Bacc("TRN2", target_bir_lowering=False, num_devices=1)
    args = [nc.dram_tensor(n, a.shape, mybir.dt.from_np(a.dtype), kind="ExternalInput").ap()
            for n, a in arrays.items()]
    out = nc.dram_tensor("out", (BATCHES, T, D), FP32, kind="ExternalOutput").ap()
    build(nc, *args, out)
    result = run_bass_kernel_spmd(nc, [arrays], core_ids=[0])
    return result.results[0]["out"]
```
